# Optimizing a Trainium2 kernel written in Bass

```python
import numpy as np
import jax
import jax.numpy as jnp

def _softmax(x, axis=-1):
    return jax.nn.softmax(x, axis=axis)

def _gelu(x):
    return jax.nn.gelu(x, approximate=True)

def _silu(x):
    return jax.nn.silu(x)

def _sigmoid(x):
    return jax.nn.sigmoid(x)

def _layernorm(x, axis=-1, eps=1e-05):
    m = jnp.mean(x, axis=axis, keepdims=True)
    v = jnp.var(x, axis=axis, keepdims=True)
    return (x - m) / jnp.sqrt(v + eps)

def _scatter_add(tgt, idx, src, axis=0):
    return tgt.at[idx].add(src)

def _segment_sum(src, seg, n):
    return jax.ops.segment_sum(src, seg, n)
kernel_name = 'mk_prb_d2_jaxref_r8_d4ea92'

def setup_inputs(seed: int=0):
    np.random.seed(seed)
    _w = jnp.asarray

    def _L0_attn_setup():
        import jax, jax.numpy as jnp
        import numpy as np
        B, T, H, S, F, G = (2, 256, 512, 128, 1248, 6)
        GRAD_ORDER_MIN = 4
        THD = 2.5
        key = jax.random.key(seed)
        ks = jax.random.split(key, 9)
        sc = 0.02
        hidden_states = jax.random.normal(ks[0], (B, T, H), jnp.float32)
        up_w = jax.random.normal(ks[1], (S, H), jnp.float32) * sc
        gate_w = jax.random.normal(ks[2], (S, H), jnp.float32) / np.sqrt(H)
        local_point = jax.random.normal(ks[3], (S,), jnp.float32)
        local_approx_output = jax.random.normal(ks[4], (H, S), jnp.float32) * sc
        fuse_weight = jax.random.normal(ks[5], (H, S, G), jnp.float32) * sc
        discount_factor = jnp.asarray(np.cumsum(np.log(np.arange(1, G + 1, dtype=np.float64))), jnp.float32)
        ffn_gate_w = jax.random.normal(ks[6], (F, H), jnp.float32) * sc
        ffn_up_w = jax.random.normal(ks[7], (F, H), jnp.float32) * sc
        ffn_down_w = jax.random.normal(ks[8], (H, F), jnp.float32) * sc
        return {'hidden_states': hidden_states, 'up_w': up_w, 'gate_w': gate_w, 'local_point': local_point, 'local_approx_output': local_approx_output, 'fuse_weight': fuse_weight, 'discount_factor': discount_factor, 'ffn_gate_w': ffn_gate_w, 'ffn_up_w': ffn_up_w, 'ffn_down_w': ffn_down_w}
    _L0_attn_in = _L0_attn_setup()

    def _L0_ffn_setup():
        import jax, jax.numpy as jnp
        import numpy as np

        def sparsemax(z):
            E = z.shape[-1]
            z_sorted = -jnp.sort(-z, axis=-1)
            z_cum = jnp.cumsum(z_sorted, axis=-1)
            k = jnp.arange(1, E + 1, dtype=z.dtype)
            support = 1.0 + k * z_sorted > z_cum
            k_z = jnp.sum(support, axis=-1, keepdims=True)
            tau_sum = jnp.take_along_axis(z_cum, k_z.astype(jnp.int32) - 1, axis=-1)
            tau = (tau_sum - 1.0) / k_z.astype(z.dtype)
            return jnp.maximum(z - tau, 0.0)
        key = jax.random.key(seed)
        ks = jax.random.split(key, 6)
        B, S, D_IN, D_OUT, E, R = (8, 256, 512, 512, 8, 16)
        x = jax.random.normal(ks[0], (B, S, D_IN), dtype=jnp.float32)
        W_base = jax.random.normal(ks[1], (D_OUT, D_IN), dtype=jnp.float32) * D_IN ** (-0.5)
        b_base = jax.random.normal(ks[2], (D_OUT,), dtype=jnp.float32) * 0.01
        W_router = jax.random.normal(ks[3], (E, D_IN), dtype=jnp.float32) * D_IN ** (-0.5)
        b_router = jnp.zeros((E,), dtype=jnp.float32)
        lora_A = jax.random.normal(ks[4], (E, D_IN, R), dtype=jnp.float32) * D_IN ** (-0.5)
        lora_B = jnp.zeros((E, R, D_OUT), dtype=jnp.float32)
        return {'x': x, 'W_base': W_base, 'b_base': b_base, 'W_router': W_router, 'b_router': b_router, 'lora_A': lora_A, 'lora_B': lora_B}
    _L0_ffn_in = _L0_ffn_setup()

    def _L1_attn_setup():
        import jax, jax.numpy as jnp
        import numpy as np
        H = 512
        D_IN = 1024
        N = 16
        K = 4
        R = 32
        EPS = 1e-06

        def rms_forward(x, eps=EPS):
            xf = x.astype(jnp.float32)
            var = jnp.mean(xf * xf, axis=-1, keepdims=True)
            return (xf * jax.lax.rsqrt(var + eps)).astype(x.dtype)
        key = jax.random.key(seed)
        ks = jax.random.split(key, 10)
        s = 0.02
        hidden_states = jax.random.normal(ks[0], (2, 128, H), dtype=jnp.float32)
        W_in = jax.random.normal(ks[1], (2 * D_IN, H), dtype=jnp.float32) * s
        conv_w = jax.random.normal(ks[2], (D_IN, K), dtype=jnp.float32) * 0.2
        conv_b = jax.random.normal(ks[3], (D_IN,), dtype=jnp.float32) * 0.02
        W_x = jax.random.normal(ks[4], (R + 2 * N, D_IN), dtype=jnp.float32) * s
        W_dt = jax.random.normal(ks[5], (D_IN, R), dtype=jnp.float32) * s
        b_dt = jax.random.normal(ks[6], (D_IN,), dtype=jnp.float32) * 0.02
        A_log = jnp.log(jnp.broadcast_to(jnp.arange(1, N + 1, dtype=jnp.float32)[None, :], (D_IN, N)))
        D = jnp.ones((D_IN,), dtype=jnp.float32)
        W_out = jax.random.normal(ks[7], (H, D_IN), dtype=jnp.float32) * s
        return {'hidden_states': hidden_states, 'W_in': W_in, 'conv_w': conv_w, 'conv_b': conv_b, 'W_x': W_x, 'W_dt': W_dt, 'b_dt': b_dt, 'A_log': A_log, 'D': D, 'W_out': W_out}
    _L1_attn_in = _L1_attn_setup()

    def _L1_ffn_setup():
        import jax, jax.numpy as jnp
        import numpy as np
        FEATURE_IN = 512
        FEATURE_OUT = 512
        R = 16
        ALPHA = 32.0
        key = jax.random.key(seed)
        k_x, k_w, k_b, k_a = jax.random.split(key, 4)
        x = jax.random.normal(k_x, (4, 256, FEATURE_IN), dtype=jnp.float32)
        bound = 1.0 / np.sqrt(FEATURE_IN)
        w = jax.random.uniform(k_w, (FEATURE_OUT, FEATURE_IN), dtype=jnp.float32, minval=-bound, maxval=bound)
        b = jax.random.uniform(k_b, (FEATURE_OUT,), dtype=jnp.float32, minval=-bound, maxval=bound)
        gain = np.sqrt(2.0 / (1.0 + 5.0 ** 2))
        bound_a = gain * np.sqrt(3.0 / FEATURE_IN)
        lora_a = jax.random.uniform(k_a, (FEATURE_IN, R), dtype=jnp.float32, minval=-bound_a, maxval=bound_a)
        lora_b = jax.random.normal(jax.random.fold_in(key, 7), (R, FEATURE_OUT), dtype=jnp.float32) * 0.01
        return {'x': x, 'w': w, 'b': b, 'lora_a': lora_a, 'lora_b': lora_b}
    _L1_ffn_in = _L1_ffn_setup()
    _d = {'L0_attn_hidden_states': _L0_attn_in['hidden_states'], 'L0_attn_up_w': _L0_attn_in['up_w'], 'L0_attn_gate_w': _L0_attn_in['gate_w'], 'L0_attn_local_point': _L0_attn_in['local_point'], 'L0_attn_local_approx_output': _L0_attn_in['local_approx_output'], 'L0_attn_fuse_weight': _L0_attn_in['fuse_weight'], 'L0_attn_discount_factor': _L0_attn_in['discount_factor'], 'L0_attn_ffn_gate_w': _L0_attn_in['ffn_gate_w'], 'L0_attn_ffn_up_w': _L0_attn_in['ffn_up_w'], 'L0_attn_ffn_down_w': _L0_attn_in['ffn_down_w'], 'L0_ffn_W_base': _L0_ffn_in['W_base'], 'L0_ffn_b_base': _L0_ffn_in['b_base'], 'L0_ffn_W_router': _L0_ffn_in['W_router'], 'L0_ffn_b_router': _L0_ffn_in['b_router'], 'L0_ffn_lora_A': _L0_ffn_in['lora_A'], 'L0_ffn_lora_B': _L0_ffn_in['lora_B'], 'L1_attn_W_in': _L1_attn_in['W_in'], 'L1_attn_conv_w': _L1_attn_in['conv_w'], 'L1_attn_conv_b': _L1_attn_in['conv_b'], 'L1_attn_W_x': _L1_attn_in['W_x'], 'L1_attn_W_dt': _L1_attn_in['W_dt'], 'L1_attn_b_dt': _L1_attn_in['b_dt'], 'L1_attn_A_log': _L1_attn_in['A_log'], 'L1_attn_D': _L1_attn_in['D'], 'L1_attn_W_out': _L1_attn_in['W_out'], 'L1_ffn_w': _L1_ffn_in['w'], 'L1_ffn_b': _L1_ffn_in['b'], 'L1_ffn_lora_a': _L1_ffn_in['lora_a'], 'L1_ffn_lora_b': _L1_ffn_in['lora_b']}
    _x0 = _d['L0_attn_hidden_states']
    _d['L0_attn_hidden_states'] = jax.random.normal(jax.random.fold_in(jax.random.key(seed), 1), (1, 1024, 512), dtype=_x0.dtype)
    del _x0
    return _d

def reference(L0_attn_hidden_states, L0_attn_up_w, L0_attn_gate_w, L0_attn_local_point, L0_attn_local_approx_output, L0_attn_fuse_weight, L0_attn_discount_factor, L0_attn_ffn_gate_w, L0_attn_ffn_up_w, L0_attn_ffn_down_w, L0_ffn_W_base, L0_ffn_b_base, L0_ffn_W_router, L0_ffn_b_router, L0_ffn_lora_A, L0_ffn_lora_B, L1_attn_W_in, L1_attn_conv_w, L1_attn_conv_b, L1_attn_W_x, L1_attn_W_dt, L1_attn_b_dt, L1_attn_A_log, L1_attn_D, L1_attn_W_out, L1_ffn_w, L1_ffn_b, L1_ffn_lora_a, L1_ffn_lora_b):

    def _L0_attn_ref(hidden_states, up_w, gate_w, local_point, local_approx_output, fuse_weight, discount_factor, ffn_gate_w, ffn_up_w, ffn_down_w):
        import jax, jax.numpy as jnp
        import numpy as np
        B, T, H, S, F, G = (2, 256, 512, 128, 1248, 6)
        GRAD_ORDER_MIN = 4
        THD = 2.5
        approx_up = hidden_states @ up_w.T
        gate_pre = hidden_states @ gate_w.T
        delta = gate_pre - local_point
        neg_factor = jnp.where(delta > 0, 1.0, -1.0).astype(hidden_states.dtype)
        delta_abs = jnp.abs(delta)
        log_delta = jnp.log(delta_abs)
        keep = (delta_abs <= THD).astype(hidden_states.dtype)
        approx_out = approx_up @ local_approx_output.T
        for idx in range(G):
            m = idx + 1
            dterm = jnp.exp(log_delta * m - discount_factor[idx])
            if m % 2 == 1:
                dterm = dterm * neg_factor
            tmp = dterm * approx_up
            if m > GRAD_ORDER_MIN:
                tmp = tmp * keep
            approx_out = approx_out + tmp @ fuse_weight[:, :, idx].T
        ffn_out = jax.nn.silu(hidden_states @ ffn_gate_w.T) * (hidden_states @ ffn_up_w.T) @ ffn_down_w.T
        return approx_out + ffn_out

    def _L0_ffn_ref(x, W_base, b_base, W_router, b_router, lora_A, lora_B):
        import jax, jax.numpy as jnp
        import numpy as np

        def sparsemax(z):
            E = z.shape[-1]
            z_sorted = -jnp.sort(-z, axis=-1)
            z_cum = jnp.cumsum(z_sorted, axis=-1)
            k = jnp.arange(1, E + 1, dtype=z.dtype)
            support = 1.0 + k * z_sorted > z_cum
            k_z = jnp.sum(support, axis=-1, keepdims=True)
            tau_sum = jnp.take_along_axis(z_cum, k_z.astype(jnp.int32) - 1, axis=-1)
            tau = (tau_sum - 1.0) / k_z.astype(z.dtype)
            return jnp.maximum(z - tau, 0.0)
        base_out = jnp.einsum('bsd,od->bso', x, W_base) + b_base
        logits = jnp.einsum('bsd,ed->bse', x, W_router) + b_router
        weights = sparsemax(logits)
        h = jnp.einsum('bsd,edr->bser', x, lora_A)
        expert_out = jnp.einsum('bser,bse,ero->bso', h, weights, lora_B)
        return base_out + expert_out

    def _L1_attn_ref(hidden_states, W_in, conv_w, conv_b, W_x, W_dt, b_dt, A_log, D, W_out):
        import jax, jax.numpy as jnp
        import numpy as np
        H = 512
        D_IN = 1024
        N = 16
        K = 4
        R = 32
        EPS = 1e-06

        def rms_forward(x, eps=EPS):
            xf = x.astype(jnp.float32)
            var = jnp.mean(xf * xf, axis=-1, keepdims=True)
            return (xf * jax.lax.rsqrt(var + eps)).astype(x.dtype)
        b, L, _ = hidden_states.shape
        proj = hidden_states @ W_in.T
        x, gate = (proj[..., :D_IN], proj[..., D_IN:])
        xpad = jnp.pad(x, ((0, 0), (K - 1, 0), (0, 0)))
        xc = conv_b
        for j in range(K):
            xc = xc + conv_w[:, j] * xpad[:, j:j + L, :]
        x = jax.nn.silu(xc)
        ssm = x @ W_x.T
        ts, Bm, Cm = (ssm[..., :R], ssm[..., R:R + N], ssm[..., R + N:])
        ts = rms_forward(ts)
        Bm = rms_forward(Bm)
        Cm = rms_forward(Cm)
        dt = jax.nn.softplus(ts @ W_dt.T + b_dt)
        A = -jnp.exp(A_log.astype(jnp.float32))

        def step(state, inp):
            dt_t, B_t, C_t, u_t = inp
            dA = jnp.exp(dt_t[..., None] * A)
            state = state * dA + (dt_t * u_t)[..., None] * B_t[:, None, :]
            y = jnp.einsum('bdn,bn->bd', state, C_t)
            return (state, y)
        init = jnp.zeros((b, D_IN, N), dtype=jnp.float32)
        xs = (dt.transpose(1, 0, 2), Bm.transpose(1, 0, 2), Cm.transpose(1, 0, 2), x.transpose(1, 0, 2))
        _, ys = jax.lax.scan(step, init, xs)
        y = ys.transpose(1, 0, 2) + x * D
        y = y * jax.nn.silu(gate)
        return y @ W_out.T

    def _L1_ffn_ref(x, w, b, lora_a, lora_b):
        import jax, jax.numpy as jnp
        import numpy as np
        FEATURE_IN = 512
        FEATURE_OUT = 512
        R = 16
        ALPHA = 32.0
        output1 = jnp.einsum('bsi,oi->bso', x, w) + b
        ab = jnp.matmul(lora_a, lora_b)
        output2 = jnp.matmul(x, ab) * (ALPHA / R)
        return output2 + output1
    x = L0_attn_hidden_states
    xn = _layernorm(x, axis=-1)
    x = x + _L0_attn_ref(xn, L0_attn_up_w, L0_attn_gate_w, L0_attn_local_point, L0_attn_local_approx_output, L0_attn_fuse_weight, L0_attn_discount_factor, L0_attn_ffn_gate_w, L0_attn_ffn_up_w, L0_attn_ffn_down_w) + _L0_ffn_ref(xn, L0_ffn_W_base, L0_ffn_b_base, L0_ffn_W_router, L0_ffn_b_router, L0_ffn_lora_A, L0_ffn_lora_B)
    xn = _layernorm(x, axis=-1)
    x = x + _L1_attn_ref(xn, L1_attn_W_in, L1_attn_conv_w, L1_attn_conv_b, L1_attn_W_x, L1_attn_W_dt, L1_attn_b_dt, L1_attn_A_log, L1_attn_D, L1_attn_W_out) + _L1_ffn_ref(xn, L1_ffn_w, L1_ffn_b, L1_ffn_lora_a, L1_ffn_lora_b)
    return x

_drawn_inputs = setup_inputs


def setup_inputs(seed=0):
    import zlib

    import numpy as np

    out = dict(_drawn_inputs(seed))
    spreads = {'L0_ffn_b_router': (0.0, 0.639), 'L0_ffn_lora_B': (0.0, 0.1), 'L1_attn_D': (1.0, 0.6)}
    factors = {'L0_ffn_b_base': 8.0,
     'L1_attn_conv_b': 8.0,
     'L1_attn_W_dt': 27.26,
     'L1_attn_b_dt': 64.0,
     'L1_attn_A_log': 64.0,
     'L1_ffn_b': 4.558,
     'L1_ffn_lora_a': 5.266,
     'L1_ffn_lora_b': 5.287}
    for name, (base, spread) in spreads.items():
        noise = np.random.default_rng([zlib.crc32(name.encode()), seed]).standard_normal(out[name].shape)
        drawn = base * np.exp(spread * noise) if base else spread * noise
        out[name] = jnp.asarray(drawn.astype(out[name].dtype))
    for name, factor in factors.items():
        out[name] = (out[name] * factor).astype(out[name].dtype)
    return out
```

```python
from contextlib import ExitStack

import concourse.bass as bass
from concourse import mybir

F32 = mybir.dt.float32
ALU = mybir.AluOpType
ACT = mybir.ActivationFunctionType
AX_X = mybir.AxisListType.X

P = 128
T = 1024
TB = 256
NB = T // TB
TC = TB // P
H = 512
KH = H // P
F = 1280
NF = F // P
G = 6
MIN_ORDER = 4
THD = 2.5
E, R0 = 8, 16
DI = 1024
NJ = DI // P
NS = 16
NH = NS // 2
NK = 2 * NJ
KC = 4
RT = 32
RX = 16
LORA_SCALE = 2.0
A_LOG_MAX = 80.0
SP_OPS = 10
FLOOR = -40.0

CW = 1024
UPG, BASE, GU, WXP, F1, WO, WX = 0, 1, 3, 13, 14, 16, 20
NCHUNK = 24
RING = 4

C_LORA_A, C_LORA_B, C_LAO, C_FUSE = 0, 512, 1024, 1536
C_ROUTER = C_FUSE + G * H
C_ALOG = C_ROUTER + KH * E
C_LA1 = C_ALOG + NJ * NS
C_VEC = C_LA1 + KH * RX
V_LP, V_B0, V_CW, V_CB, V_BDT, V_D, V_B1 = 0, 1, 5, 37, 45, 53, 61
V_DISC, V_BR = 65, 71
NRES = C_VEC + V_BR + E

K_ID, K_MEAN, K_RMS, K_INV, K_EPS = 0, 128, 256, 384, 392
NCONST = 394


def scan_order():
    slots = []
    for k in range(NK):
        j, early, late = k // 2, [], []
        early.append(("add0", k))
        if k % 2 == 0 and j + 1 < NJ:
            early.append(("dg_a", j + 1))
        if k + 1 < NK:
            early += [("exp", k + 1), ("mul", k + 1)]
        early += [("scan", k), ("cmul", k)]
        if k % 2 == 0 and j + 1 < NJ:
            late += [("dg_b", j + 1), ("dg_c", j + 1)]
        if k >= 2:
            late.append(("red", k - 2))
            if k % 2:
                late.append(("fin", (k - 3) // 2))
        slots.append((early, late))
    slots.append(([("red", NK - 2), ("red", NK - 1), ("fin", NJ - 1)], []))
    return slots


def layer0_order():
    out = [("mean0", 0, 4), ("var0", 0, 4), ("router", 0, 4), ("updelta", 0, 8), ("lora", 0, 4), ("power", 0, 0),
           ("experts", 0, 2), ("gu", 0, 8), ("base", 0, 16), ("gu", 1, 8), ("hmul", 0, 0)]
    for f in range(NF):
        out.append(("down", f, 4))
        if f + 2 < NF:
            out.append(("gu", f + 2, 8))
        if f + 1 < NF:
            out.append(("hmul", f + 1, 0))
    out += [("taylor", 0, 28), ("loraout", 0, 4), ("x1", 0, 0)]
    return out


def phase_a(with_layer0):
    slots, rest = scan_order(), layer0_order() if with_layer0 else []
    total, done, out = sum(w for _, _, w in rest) or 1, 0, []
    for k, (early, late) in enumerate(slots):
        out += early
        while rest and (done < total * (k + 1) / NK or k >= NK - 1):
            s, i, w = rest.pop(0)
            done += w
            out.append(("next", s, i))
        out += late
    return out


def pre_order():
    out = []
    for c in range(4):
        out.append(("winx", c))
        if c:
            out.append(("conv", c - 1))
        if c > 1:
            out.append(("csilu", c - 2))
    out += [("conv", 3), ("csilu", 2), ("csilu", 3), ("wx", 0), ("rms", 0), ("dg_a", 0)]
    out += [("bc", i) for i in range(4)] + [("dg_b", 0), ("dg_c", 0)] + [("bc", i) for i in range(4, 8)]
    out += [("keepx", 0)]
    out += [("exp", 0), ("mul", 0)] + [("bc", i) for i in range(8, 16)]
    return out


PROLOGUE = ([("next", s, i) for s, i, _ in layer0_order()] + [("next", "mean1", 0), ("next", "var1", 0)]
            + [("next",) + s for s in pre_order()])
OUT_STEPS = [("ffn1a", 0), ("ffn1", 0), ("next", "mean1", 0), ("wout", 0), ("wout", 1), ("next", "var1", 0),
             ("wout", 2), ("wout", 3), ("out", 0)]
BODY = ([("next", "xload", 0)] + phase_a(True) + OUT_STEPS + [("next",) + s for s in pre_order()] + [("store", 0)])
LAST = phase_a(False) + [s for s in OUT_STEPS if s[0] != "next"] + [("store", 0)]


def streamed(order):
    out = []
    for s in order:
        nxt = s[0] == "next"
        s, i = (s[1:] if nxt else s)[:2]
        if s in ("updelta", "wx"):
            out.append(({"updelta": UPG, "wx": WXP}[s], 0, nxt))
        elif s in ("base", "ffn1"):
            out += [({"base": BASE, "ffn1": F1}[s], kk, nxt) for kk in range(2)]
        elif s in ("gu", "wout", "winx"):
            out.append(({"gu": GU, "wout": WO, "winx": WX}[s], i, nxt))
        elif s in ("down", "dg_a"):
            out.append((s, i, nxt))
    return out


def in_ring(order):
    return [c for c in streamed(order) if c[0] not in ("down", "dg_a")]


def run(eng, step):
    def stretch(order, first, b, turns):
        n = first
        for s in order:
            nxt = s[0] == "next"
            step(s[-2], s[-1], b + 1 if nxt else b, (n, turns))
            n += len(in_ring([s]))

    stretch(PROLOGUE, 0, -1, 0)
    stretch(BODY, N0, 0, 0)
    with eng.Fori(1, NB - 1) as b:
        stretch(BODY, N0, b, b)
    stretch(LAST, N0 + N1 * (NB - 1), NB - 1, 0)


N0, N1 = len(in_ring(PROLOGUE)), len(in_ring(BODY))
assert N1 % RING == 0


def bc_rows(i):
    part, r = i // 4, 2 * (i % 4)
    return (part // 2) * NH + r, part % 2


def after(eng, sem, n):
    if not isinstance(n, int) or n > 0:
        eng.wait_ge(sem, n)


def build(nc, xT, chunks, down_w, gate_w, res, wdt, lb1, consts, outT):
    with ExitStack() as ctx:
        def sb(name, shape):
            return ctx.enter_context(nc.sbuf_tensor(name, shape, F32))

        def bank(name, shape=(P, 2, TB)):
            return ctx.enter_context(nc.psum_tensor(name, list(shape), F32))

        def sem(name):
            return ctx.enter_context(nc.semaphore(name))

        ring = sb("ring", [P, RING, CW])
        resw = sb("resw", [P, NRES])
        down_sb = sb("down_sb", [P, 2, H])
        gate_sb = sb("gate_sb", [P, 2, H])
        wdt_sb = sb("wdt_sb", [RT, DI])
        lb1_sb = sb("lb1_sb", [RX, H])
        cst = sb("cst", [P, NCONST])
        negA = sb("negA", [P, NJ, NS])
        cm = sb("cm", [P, G])
        nlp = sb("nlp", [P, 1])
        ones8 = sb("ones8", [P, E])
        cum = sb("cum", [P, TC, E])
        x_sb = sb("x_sb", [P, KH, TB])
        xn0 = sb("xn0", [P, KH, TB])
        sq = sb("sq", [P, KH, TB])
        rstd = sb("rstd", [P, TB])
        up = sb("up", [P, TB])
        delta = sb("delta", [P, TB])
        keep = sb("keep", [P, TB])
        q = sb("q", [P, G, TB])
        z8 = sb("z8", [P, TC, E])
        zs = sb("zs", [P, TC, E])
        tau = sb("tau", [P, TC])
        wrep = sb("wrep", [P, TC, P])
        hw = sb("hw", [P, TB])
        gcl = sb("gcl", [P, 2, TB])
        sig = sb("sig", [P, 2, TB])
        h = sb("h", [P, 3, TB])
        xres = sb("xres", [P, KH, TB])
        xn1 = sb("xn1", [P, KH, TB])
        xpad = sb("xpad", [P, NJ, TB + KC - 1])
        u = sb("u", [P, NJ, TB])
        bct = sb("bct", [P, TB])
        Bb = sb("Bb", [P, NS, TB])
        Cb = sb("Cb", [P, NS, TB])
        xb = sb("xb", [P, TB])
        ee = sb("ee", [P, TB])
        ww = sb("ww", [P, TB])
        gs = sb("gs", [P, TB])
        gg = sb("gg", [P, 3, TB])
        dt = sb("dt", [P, 2, TB])
        du = sb("du", [P, 2, TB])
        e0 = sb("e0", [P, 2, NS])
        c0 = sb("c0", [P, 2, NH])
        hprev = sb("hprev", [P, NJ, NS])
        dA = sb("dA", [P, 2, NH, TB])
        bs = sb("bs", [P, 4, NH, TB])
        fa = sb("fa", [P, TB])
        ha = sb("ha", [RX, TB])

        cv, cs = q[:, 0:4, :], sig
        ssm, rr = h[:, 0, :], h[:, 1, :]

        def vec(i, rows=P):
            return resw[0:rows, C_VEC + i:C_VEC + i + 1]

        ident = cst[:, K_ID:K_ID + P]
        mean_w = cst[:, K_MEAN:K_MEAN + P]
        rms_w = cst[:, K_RMS:K_RMS + P]
        inv_k = cst[:, K_INV:K_INV + E]
        lora_a = resw[:, C_LORA_A:C_LORA_A + KH * P].rearrange("p (k m) -> p k m", k=KH)
        lora_b = resw[:, C_LORA_B:C_LORA_B + H]
        lao = resw[:, C_LAO:C_LAO + H]
        fuse = resw[:, C_FUSE:C_FUSE + G * H].rearrange("p (g m) -> p g m", g=G)
        router = resw[:, C_ROUTER:C_ROUTER + KH * E].rearrange("p (k m) -> p k m", k=KH)
        a_log = resw[:, C_ALOG:C_ALOG + NJ * NS]
        la1 = resw[:, C_LA1:C_LA1 + KH * RX].rearrange("p (k m) -> p k m", k=KH)
        disc = resw[:, C_VEC + V_DISC:C_VEC + V_DISC + G]
        b_router = resw[:, C_VEC + V_BR:C_VEC + V_BR + E]

        pair = [bank("pair0"), bank("pair1")]
        acc = [bank("acc0"), bank("acc1")]
        ybank = bank("ybank")
        small = bank("small")
        side = [bank("side0"), bank("side1")]

        s_res, s_setup_act, s_setup_dve = sem("s_res"), sem("s_setup_act"), sem("s_setup_dve")
        s_chunk = [sem(f"s_chunk{i}") for i in range(RING)]
        s_downw = [sem("s_downw0"), sem("s_downw1")]
        s_gatew = [sem("s_gatew0"), sem("s_gatew1")]
        s_basew, s_f1w, s_wo = sem("s_basew"), sem("s_f1w"), sem("s_wo")
        s_x = sem("s_x")
        s_mean = [sem("s_mean0"), sem("s_mean1")]
        s_xc = [sem("s_xc0"), sem("s_xc1")]
        s_sq = [sem("s_sq0"), sem("s_sq1")]
        s_var = [sem("s_var0"), sem("s_var1")]
        s_rstd = [sem("s_rstd0"), sem("s_rstd1")]
        s_xn = [sem("s_xn0"), sem("s_xn1")]
        s_router, s_sparse = sem("s_router"), sem("s_sparse")
        s_ud, s_uds, s_pow, s_tay = sem("s_ud"), sem("s_uds"), sem("s_pow"), sem("s_tay")
        s_lora, s_wt, s_hw = sem("s_lora"), sem("s_wt"), sem("s_hw")
        s_gu, s_gcl, s_sig, s_silu, s_h, s_down = (sem("s_gu"), sem("s_gcl"), sem("s_sig"), sem("s_silu"),
                                                  sem("s_h"), sem("s_down"))
        s_acc0, s_x1, s_keepx = sem("s_acc0"), sem("s_x1"), sem("s_keepx")
        s_winx, s_xpad, s_conv, s_csig, s_u, s_halo = (sem("s_winx"), sem("s_xpad"), sem("s_conv"), sem("s_csig"),
                                                       sem("s_u"), sem("s_halo"))
        s_ssm, s_ssq, s_rms, s_rr, s_bct = sem("s_ssm"), sem("s_ssq"), sem("s_rms"), sem("s_rr"), sem("s_bct")
        s_bc, s_bce = sem("s_bc"), sem("s_bce")
        s_dg, s_xb, s_gcg, s_e, s_w, s_ln, s_m = (sem("s_dg"), sem("s_xb"), sem("s_gcg"), sem("s_e"), sem("s_w"),
                                                  sem("s_ln"), sem("s_m"))
        s_dt, s_du, s_gsig, s_gg = sem("s_dt"), sem("s_du"), sem("s_gsig"), sem("s_gg")
        s_e0, s_exp, s_c0, s_mul, s_add0, s_scan, s_hprev, s_cmul, s_red, s_fa, s_z = (
            sem("s_e0"), sem("s_exp"), sem("s_c0"), sem("s_mul"), sem("s_add0"), sem("s_scan"), sem("s_hprev"),
            sem("s_cmul"), sem("s_red"), sem("s_fa"), sem("s_z"))
        s_ffn1a, s_ha, s_ffn1, s_acc1, s_out, s_store = (sem("s_ffn1a"), sem("s_ha"), sem("s_ffn1"), sem("s_acc1"),
                                                         sem("s_out"), sem("s_store"))
        NRESDMA = 4

        block = ctx.enter_context(nc.Block())

        @block.sync
        def _(sp):
            def ring_used(kind, i, c):
                sem_, n = {UPG: (s_ud, c + 1), BASE: (s_basew, 2 * c + i + 1), GU: (s_gu, NF * c + i + 1),
                           WXP: (s_ssm, c + 1), F1: (s_f1w, 2 * c + i + 1), WO: (s_wo, 4 * c + i + 1),
                           WX: (s_winx, 4 * c + i + 1)}[kind]
                sp.wait_ge(sem_, n)

            def load(order, first, b, before):
                ahead = list(before)
                for kind, i, nxt in streamed(order):
                    c = b + 1 if nxt else b
                    if kind == "down":
                        after(sp, s_down, NF * c + i - 1)
                        sp.dma_start(down_sb[:, i % 2, :], down_w[i]).then_inc(s_downw[i % 2], 16)
                    elif kind == "dg_a":
                        after(sp, s_dg, NJ * c + i - 1)
                        sp.dma_start(gate_sb[:, i % 2, :], gate_w[i]).then_inc(s_gatew[i % 2], 16)
                    else:
                        if len(ahead) >= RING:
                            ring_used(*ahead[-RING])
                        slot = first % RING
                        sp.dma_start(ring[:, slot, :], chunks[kind + i]).then_inc(s_chunk[slot], 16)
                        ahead.append((kind, i, c))
                        first += 1

            def tail(order, b):
                return [(kind, i, b + 1 if nxt else b) for kind, i, nxt in in_ring(order)][-RING:]

            sp.dma_start(x_sb[:, :, :], xT[:, :, 0:TB]).then_inc(s_x, 16)
            sp.dma_start(cst[:, :], consts).then_inc(s_res, 16)
            sp.dma_start(resw[:, :], res).then_inc(s_res, 16)
            sp.dma_start(wdt_sb[:, :], wdt).then_inc(s_res, 16)
            sp.dma_start(lb1_sb[:, :], lb1).then_inc(s_res, 16)
            load(PROLOGUE, 0, -1, [])
            load(BODY, N0, 0, tail(BODY, -1))
            with sp.Fori(1, NB - 1) as b:
                load(BODY, N0, b, tail(BODY, b - 1))
            load(LAST, N0 + N1 * (NB - 1), NB - 1, tail(BODY, NB - 2))
            sp.wait_ge(s_store, 16 * NB)

        @block.tensor
        def _(pe):
            pe.wait_ge(s_res, 16 * NRESDMA)
            def chunk(n, more=0):
                at = n[0] + more
                pe.wait_ge(s_chunk[at % RING], 16 * (at // RING + 1) + 16 * (N1 // RING) * n[1])
                return ring[:, at % RING, :]

            def mm(out, w, x, start, stop):
                return nc.tensor.matmul(out, w, x, start=start, stop=stop, skip_group_check=True)

            def norm_sum(l, c, out, src):
                for k in range(KH):
                    m = mm(out, mean_w, src[:, k, :], k == 0, k == KH - 1)
                return m

            def step(s, i, c, t):
                if s in ("mean0", "mean1"):
                    l = int(s[-1])
                    src = x_sb
                    if l == 0:
                        pe.wait_ge(s_x, 16 * c + 16)
                        after(pe, s_bct, c)
                    else:
                        pe.wait_ge(s_x1, KH * c + KH)
                        after(pe, s_ha, c)
                    norm_sum(l, c, small[:, 0, :], src).then_inc(s_mean[l], 1)
                elif s in ("var0", "var1"):
                    l = int(s[-1])
                    pe.wait_ge(s_sq[l], c + 1)
                    norm_sum(l, c, small[:, 1, :], sq).then_inc(s_var[l], 1)
                elif s == "router":
                    pe.wait_ge(s_xn[0], c + 1)
                    for tc in range(TC):
                        for k in range(KH):
                            m = mm(small[:, 0, tc * E:(tc + 1) * E], xn0[:, k, tc * P:(tc + 1) * P],
                                   router[:, k, :], k == 0, k == KH - 1)
                    m.then_inc(s_router, 1)
                elif s == "updelta":
                    after(pe, s_bce, NK * c)
                    w = chunk(t).rearrange("p (k m) -> p k m", k=KH)
                    for half in range(2):
                        for k in range(KH):
                            m = mm(pair[0][:, half, :], w[:, k, half * P:(half + 1) * P], xn0[:, k, :],
                                   k == 0, k == KH - 1)
                    m.then_inc(s_ud, 1)
                elif s == "lora":
                    for k in range(KH):
                        m = mm(pair[1][:, 1, :], lora_a[:, k, :], xn0[:, k, :], k == 0, k == KH - 1)
                elif s == "experts":
                    pe.wait_ge(s_sparse, SP_OPS * c + SP_OPS)
                    for tc in range(TC):
                        m = nc.tensor.matmul(pair[1][:, 0, tc * P:(tc + 1) * P], wrep[:, tc, :], ident,
                                             start=True, stop=True, is_transpose=True, skip_group_check=True)
                    m.then_inc(s_lora, 1)
                elif s == "gu":
                    if i == 0:
                        pe.wait_ge(s_uds, 3 * c + 3)
                    elif i == 1:
                        pe.wait_ge(s_hw, c + 1)
                    else:
                        pe.wait_ge(s_h, NF * c + i - 1)
                    w = chunk(t).rearrange("p (k m) -> p k m", k=KH)
                    for half in range(2):
                        for k in range(KH):
                            m = mm(pair[i % 2][:, half, :], w[:, k, half * P:(half + 1) * P], xn0[:, k, :],
                                   k == 0, k == KH - 1)
                    m.then_inc(s_gu, 1)
                elif s == "base":
                    after(pe, s_out, KH * c - KH)
                    for kk in range(2):
                        w = chunk(t, kk).rearrange("p (k m) -> p k m", k=2)
                        for k in range(2):
                            for mt in range(KH):
                                m = mm(acc[mt // 2][:, mt % 2, :], w[:, k, mt * P:(mt + 1) * P],
                                       xn0[:, 2 * kk + k, :], kk == 0 and k == 0 and mt % 2 == 0, False)
                        m.then_inc(s_basew, 1)
                elif s == "down":
                    pe.wait_ge(s_h, NF * c + i + 1)
                    pe.wait_ge(s_downw[i % 2], 16 * (NF // 2) * c + 16 * (i // 2 + 1))
                    for mt in range(KH):
                        m = mm(acc[mt // 2][:, mt % 2, :], down_sb[:, i % 2, mt * P:(mt + 1) * P], h[:, i % 3, :],
                               False, False)
                    m.then_inc(s_down, 1)
                elif s == "taylor":
                    for mt in range(KH):
                        m = mm(acc[mt // 2][:, mt % 2, :], lao[:, mt * P:(mt + 1) * P], up[:, :], False, False)
                    pe.wait_ge(s_tay, 4 * c + 4)
                    pe.wait_ge(s_pow, 9 * c + 9)
                    for g in range(G):
                        for mt in range(KH):
                            m = mm(acc[mt // 2][:, mt % 2, :], fuse[:, g, mt * P:(mt + 1) * P], q[:, g, :],
                                   False, False)
                elif s == "loraout":
                    pe.wait_ge(s_hw, c + 1)
                    for mt in range(KH):
                        m = mm(acc[mt // 2][:, mt % 2, :], lora_b[:, mt * P:(mt + 1) * P], hw[:, :],
                               False, True)
                    m.then_inc(s_acc0, 1)
                elif s == "winx":
                    pe.wait_ge(s_xn[1], c + 1)
                    if i >= 2:
                        pe.wait_ge(s_xpad, 4 * c + i - 1)
                    else:
                        after(pe, s_gcg, NJ * c)
                    w = chunk(t).rearrange("p (k m) -> p k m", k=KH)
                    for half in range(2):
                        for k in range(KH):
                            m = mm(side[i % 2][:, half, :], w[:, k, half * P:(half + 1) * P], xn1[:, k, :],
                                   k == 0, k == KH - 1)
                    m.then_inc(s_winx, 1)
                elif s == "wx":
                    w_x = chunk(t).rearrange("p (k m) -> p k m", k=NJ)
                    for k in range(NJ):
                        pe.wait_ge(s_u, NJ * c + k + 1)
                        m = mm(small[:, 0, :], w_x[:, k, :], u[:, k, :], k == 0, k == NJ - 1)
                    m.then_inc(s_ssm, 1)
                elif s == "rms":
                    pe.wait_ge(s_ssq, 2 * c + 2)
                    mm(small[:, 1, :], rms_w, sq[:, 0, :], True, True).then_inc(s_rms, 1)
                elif s == "bc":
                    if i < 2:
                        pe.wait_ge(s_h, NF * c + NF)
                        pe.wait_ge(s_bct, c + 1)
                    else:
                        pe.wait_ge(s_bce, NK * c + i - 1)
                    for half in range(2):
                        n, which = bc_rows(i)
                        row = RT + NS * which + n + half
                        m = mm(pair[i % 2][:, half, :], cst[:, K_ID + row:K_ID + row + 1].to_broadcast([P, P]),
                               bct[:, :], True, True)
                    m.then_inc(s_bc, 1)
                elif s == "dg_a":
                    pe.wait_ge(s_bct, c + 1)
                    if i < 2:
                        pe.wait_ge(s_xpad, 4 * c + 4)
                    else:
                        pe.wait_ge(s_gcg, NJ * c + i - 1)
                        pe.wait_ge(s_xb, NJ * c + i - 1)
                    mm(side[i % 2][:, 0, :], wdt_sb[:, i * P:(i + 1) * P], bct[0:RT, :], True, True)
                    pe.wait_ge(s_gatew[i % 2], 16 * (NJ // 2) * c + 16 * (i // 2 + 1))
                    for k in range(KH):
                        m = mm(side[i % 2][:, 1, :], gate_sb[:, i % 2, k * P:(k + 1) * P], xn1[:, k, :],
                               k == 0, k == KH - 1)
                    m.then_inc(s_dg, 1)
                elif s == "red":
                    j, hn = i // 2, i % 2
                    pe.wait_ge(s_cmul, NK * c + i + 1)
                    if hn == 0:
                        after(pe, s_fa, NJ * c + j)
                    for n in range(NH):
                        m = mm(ybank[:, 0, :], ident, bs[:, i % 4, n, :], hn == 0 and n == 0,
                               hn == 1 and n == NH - 1)
                    m.then_inc(s_red, 1)
                elif s == "ffn1a":
                    for k in range(KH):
                        m = mm(small[0:RX, 0, :], la1[:, k, :], xn1[:, k, :], k == 0, k == KH - 1)
                    m.then_inc(s_ffn1a, 1)
                elif s == "ffn1":
                    if isinstance(c, int) and c == NB - 1:
                        pe.wait_ge(s_out, KH * c)
                    else:
                        pe.wait_ge(s_x1, KH * c + 2 * KH)
                    for kk in range(2):
                        w = chunk(t, kk).rearrange("p (k m) -> p k m", k=2)
                        for k in range(2):
                            for mt in range(KH):
                                m = mm(acc[mt // 2][:, mt % 2, :], w[:, k, mt * P:(mt + 1) * P],
                                       xn1[:, 2 * kk + k, :], kk == 0 and k == 0 and mt % 2 == 0, False)
                        m.then_inc(s_f1w, 1)
                    pe.wait_ge(s_ha, c + 1)
                    for mt in range(KH):
                        m = mm(acc[mt // 2][:, mt % 2, :], lb1_sb[:, mt * P:(mt + 1) * P], ha[:, :], False, False)
                    m.then_inc(s_ffn1, 1)
                elif s == "wout":
                    pe.wait_ge(s_z, NJ * c + 2 * i + 2)
                    w = chunk(t).rearrange("p (k m) -> p k m", k=2)
                    for k in range(2):
                        for mt in range(KH):
                            m = mm(acc[mt // 2][:, mt % 2, :], w[:, k, mt * P:(mt + 1) * P], u[:, 2 * i + k, :],
                                   False, i == 3 and k == 1)
                    m.then_inc(s_wo, 1)

            run(pe, step)

        @block.vector
        def _(dve):
            V = nc.vector
            V.memset(hprev[:, :, :], 0.0).then_inc(s_setup_dve, 1)
            V.memset(dA[:, :, :, 0:1], 0.0).then_inc(s_setup_dve, 1)
            V.memset(ones8[:, :], 1.0).then_inc(s_setup_dve, 1)
            V.memset(xpad[:, :, 0:KC - 1], 0.0).then_inc(s_halo, 1)
            dve.wait_ge(s_res, 16 * NRESDMA)
            V.tensor_scalar(negA[:, :, :].rearrange("p j n -> p (j n)"), a_log, A_LOG_MAX, None,
                            ALU.min).then_inc(s_setup_dve, 1)
            V.tensor_scalar(nlp[:, :], vec(V_LP), -1.0, None, ALU.mult).then_inc(s_setup_dve, 1)
            dve.wait_ge(s_setup_act, 2)
            V.tensor_scalar(negA[:, :, :], negA[:, :, :], -1.0, None, ALU.mult).then_inc(s_setup_dve, 1)

            def step(s, i, c, _n):
                if s in ("mean0", "mean1"):
                    l = int(s[-1])
                    xn = (xn0, xn1)[l]
                    dve.wait_ge(s_mean[l], c + 1)
                    if l == 1:
                        after(dve, s_ffn1, c)
                    V.tensor_tensor(xn[:, :, :], x_sb[:, :, :],
                                    small[:, 0, :].unsqueeze(1).to_broadcast([P, KH, TB]),
                                    ALU.subtract).then_inc(s_xc[l], 1)
                elif s in ("var0", "var1"):
                    l = int(s[-1])
                    xn = (xn0, xn1)[l]
                    dve.wait_ge(s_rstd[l], 2 * c + 2)
                    V.tensor_tensor(xn[:, :, :], xn[:, :, :], rstd[:, :].unsqueeze(1).to_broadcast([P, KH, TB]),
                                    ALU.mult).then_inc(s_xn[l], 1)
                elif s == "router":
                    dve.wait_ge(s_router, c + 1)
                    at = SP_OPS * c
                    V.tensor_tensor(z8[:, :, :], small[:, 0, 0:TC * E].rearrange("p (a b) -> p a b", a=TC),
                                    b_router.unsqueeze(1).to_broadcast([P, TC, E]), ALU.add).then_inc(s_sparse, 1)
                    dve.wait_ge(s_sparse, at + 1)
                    V.tensor_copy(cum[:, :, :], z8[:, :, :])
                    for tc in range(TC):
                        V.max(zs[:, tc, :], z8[:, tc, :]).then_inc(s_sparse, 1)
                    for tc in range(TC):
                        dve.wait_ge(s_sparse, at + 2 + tc)
                        V.tensor_tensor_scan(cum[:, tc, :], ones8[:, :], zs[:, tc, :], 0.0, ALU.mult,
                                             ALU.add).then_inc(s_sparse, 1)
                    dve.wait_ge(s_sparse, at + 5)
                    V.scalar_tensor_tensor(zs[:, :, :], cum[:, :, :], -1.0,
                                           inv_k.unsqueeze(1).to_broadcast([P, TC, E]), ALU.add,
                                           ALU.mult).then_inc(s_sparse, 1)
                    dve.wait_ge(s_sparse, at + 6)
                    V.tensor_reduce(tau[:, :], zs[:, :, :], AX_X, ALU.max).then_inc(s_sparse, 1)
                    dve.wait_ge(s_sparse, at + 7)
                    for tc in range(TC):
                        V.tensor_scalar(z8[:, tc, :], z8[:, tc, :], tau[:, tc:tc + 1], 0.0, ALU.subtract,
                                        ALU.max).then_inc(s_sparse, 1)
                    dve.wait_ge(s_sparse, at + 9)
                    V.tensor_copy(wrep[:, :, :].rearrange("p a (e r) -> p a e r", e=E),
                                  z8[:, :, :].unsqueeze(3).to_broadcast([P, TC, E, R0])).then_inc(s_sparse, 1)
                elif s == "power":
                    dve.wait_ge(s_uds, 3 * c + 3)
                    V.tensor_scalar(keep[:, :], keep[:, :], THD, None, ALU.is_le).then_inc(s_pow, 1)
                    for g in range(G):
                        if g:
                            dve.wait_ge(s_pow, 9 * c + g + 1)
                        V.tensor_tensor(q[:, g, :], q[:, g - 1, :] if g else up[:, :], delta[:, :],
                                        ALU.mult).then_inc(s_pow, 1)
                    for n, g in enumerate(range(MIN_ORDER, G)):
                        dve.wait_ge(s_pow, 9 * c + 7)
                        V.scalar_tensor_tensor(q[:, g, :], q[:, g, :], cm[:, g:g + 1], keep[:, :], ALU.mult,
                                               ALU.mult).then_inc(s_pow, 1)
                elif s == "experts":
                    dve.wait_ge(s_wt, c + 1)
                    V.tensor_tensor(hw[:, :], pair[1][:, 1, :], hw[:, :], ALU.mult).then_inc(s_hw, 1)
                elif s == "gu":
                    dve.wait_ge(s_gu, NF * c + i + 1)
                    after(dve, s_h, NF * c + i - 1 if i > 1 else NF * c)
                    V.tensor_scalar(gcl[:, i % 2, :], pair[i % 2][:, 0, :], FLOOR, None, ALU.max).then_inc(s_gcl, 1)
                elif s == "hmul":
                    dve.wait_ge(s_silu, NF * c + i + 1)
                    after(dve, s_down, NF * c + i - 2 if i > 2 else NF * c)
                    V.tensor_tensor(h[:, i % 3, :], gcl[:, i % 2, :], pair[i % 2][:, 1, :],
                                    ALU.mult).then_inc(s_h, 1)
                elif s == "x1":
                    dve.wait_ge(s_acc0, c + 1)
                    for mt in range(KH):
                        V.scalar_tensor_tensor(x_sb[:, mt, :], acc[mt // 2][:, mt % 2, :], vec(V_B0 + mt),
                                               x_sb[:, mt, :], ALU.add, ALU.add).then_inc(s_x1, 1)
                elif s == "conv":
                    dve.wait_ge(s_xpad, 4 * c + i + 1)
                    after(dve, s_u, NJ * c + 2 * i - 2 if i > 1 else NJ * c)
                    for tap in range(KC + 1):
                        for d in range(2):
                            j = 2 * i + d
                            acc_ = cv[:, j % 4, :]
                            if tap:
                                dve.wait_ge(s_conv, 40 * c + 10 * i + 2 * tap - 1 + d)
                            if tap == 0:
                                V.tensor_scalar(acc_, xpad[:, j, 0:TB], vec(V_CW + KC * j), vec(V_CB + j), ALU.mult,
                                                ALU.add).then_inc(s_conv, 1)
                            elif tap < KC:
                                V.scalar_tensor_tensor(acc_, xpad[:, j, tap:tap + TB], vec(V_CW + KC * j + tap),
                                                       acc_, ALU.mult, ALU.add).then_inc(s_conv, 1)
                            else:
                                V.tensor_scalar(acc_, acc_, FLOOR, None, ALU.max).then_inc(s_conv, 1)
                    if i == 3:
                        V.tensor_copy(xpad[:, :, 0:KC - 1], xpad[:, :, TB:TB + KC - 1]).then_inc(s_halo, 1)
                elif s == "rms":
                    dve.wait_ge(s_rr, 2 * c + 2)
                    V.tensor_tensor(bct[:, :], ssm, rr, ALU.mult).then_inc(s_bct, 1)
                elif s == "keepx":
                    after(dve, s_store, 16 * c)
                    V.tensor_copy(xres[:, :, :], x_sb[:, :, :]).then_inc(s_keepx, 1)
                elif s == "dg_a":
                    dve.wait_ge(s_dg, NJ * c + i + 1)
                    dve.wait_ge(s_xb, NJ * c + i + 1)
                    after(dve, s_z, NJ * c + i - 2 if i > 2 else NJ * c)
                    V.tensor_scalar(gg[:, i % 3, :], side[i % 2][:, 1, :], FLOOR, None, ALU.max).then_inc(s_gcg, 1)
                elif s == "dg_b":
                    dve.wait_ge(s_e, 2 * NJ * c + 2 * i + 2)
                    after(dve, s_m, NJ * c + i)
                    V.tensor_scalar(ww[:, :], ee[:, :], 1.0, None, ALU.add).then_inc(s_w, 1)
                    dve.wait_ge(s_w, 2 * NJ * c + 2 * i + 1)
                    V.scalar_tensor_tensor(ee[:, :], ww[:, :], -1.0, ee[:, :], ALU.add,
                                           ALU.subtract).then_inc(s_w, 1)
                elif s == "dg_c":
                    dve.wait_ge(s_ln, NJ * c + i + 1)
                    V.scalar_tensor_tensor(xb[:, :], xb[:, :], 0.0, ww[:, :], ALU.max, ALU.add).then_inc(s_m, 1)
                elif s == "mul":
                    j, hn = i // 2, i % 2
                    dve.wait_ge(s_du, NJ * c + j + 1)
                    dve.wait_ge(s_bce, NK * c + 8 * hn + 4)
                    after(dve, s_red, NK * c + i - 3 if i > 3 else NK * c)
                    V.tensor_tensor(bs[:, i % 4, :, :], Bb[:, hn * NH:hn * NH + NH, :],
                                    du[:, j % 2, :].unsqueeze(1).to_broadcast([P, NH, TB]),
                                    ALU.mult).then_inc(s_mul, 1)
                    dve.wait_ge(s_e0, NJ * c + j + 1)
                    after(dve, s_hprev, NK * c)
                    V.tensor_tensor(c0[:, i % 2, :], e0[:, j % 2, hn * NH:hn * NH + NH],
                                    hprev[:, j, hn * NH:hn * NH + NH], ALU.mult).then_inc(s_c0, 1)
                elif s == "add0":
                    dve.wait_ge(s_c0, NK * c + i + 1)
                    dve.wait_ge(s_mul, NK * c + i + 1)
                    V.tensor_tensor(bs[:, i % 4, :, 0:1], bs[:, i % 4, :, 0:1], c0[:, i % 2, :].unsqueeze(2),
                                    ALU.add).then_inc(s_add0, 1)
                elif s == "scan":
                    dve.wait_ge(s_exp, NK * c + i + 1)
                    dve.wait_ge(s_add0, NK * c + i + 1)
                    flat = bs[:, i % 4, :, :].rearrange("p n t -> p (n t)")
                    V.tensor_tensor_scan(flat, dA[:, i % 2, :, :].rearrange("p n t -> p (n t)"), flat, 0.0, ALU.mult,
                                         ALU.add).then_inc(s_scan, 1)
                    dve.wait_ge(s_scan, NK * c + i + 1)
                    V.tensor_copy(hprev[:, i // 2, (i % 2) * NH:(i % 2) * NH + NH].unsqueeze(2),
                                  bs[:, i % 4, :, TB - 1:TB]).then_inc(s_hprev, 1)
                elif s == "fin":
                    dve.wait_ge(s_red, NK * c + 2 * i + 2)
                    after(dve, s_z, NJ * c + i)
                    V.scalar_tensor_tensor(fa[:, :], u[:, i, :], vec(V_D + i), ybank[:, 0, :], ALU.mult,
                                           ALU.add).then_inc(s_fa, 1)
                    dve.wait_ge(s_fa, NJ * c + i + 1)
                    dve.wait_ge(s_gg, NJ * c + i + 1)
                    V.tensor_tensor(u[:, i, :], fa[:, :], gg[:, i % 3, :], ALU.mult).then_inc(s_z, 1)
                elif s == "out":
                    dve.wait_ge(s_wo, 4 * c + 4)
                    dve.wait_ge(s_keepx, c + 1)
                    for mt in range(KH):
                        V.scalar_tensor_tensor(xres[:, mt, :], acc[mt // 2][:, mt % 2, :], vec(V_B1 + mt),
                                               xres[:, mt, :], ALU.add, ALU.add).then_inc(s_out, 1)

            run(dve, step)

        @block.scalar
        def _(act):
            A = nc.scalar.activation
            act.preload_act_table_set("natural_log_exp_and_others")
            act.wait_ge(s_res, 16 * NRESDMA)
            A(cm[:, :], disc, ACT.Exp, scale=-1.0).then_inc(s_setup_act, 1)
            act.wait_ge(s_setup_dve, 4)
            A(negA[:, :, :], negA[:, :, :], ACT.Exp).then_inc(s_setup_act, 1)

            def sigmoid(out, src, sem_, at):
                A(out, src, ACT.Exp, scale=-1.0).then_inc(sem_, 1)
                act.wait_ge(sem_, at + 1)
                A(out, out, ACT.Ln, bias=1.0).then_inc(sem_, 1)
                act.wait_ge(sem_, at + 2)
                A(out, out, ACT.Exp, scale=-1.0).then_inc(sem_, 1)

            def step(s, i, c, _n):
                if s == "xload":
                    act.wait_ge(s_keepx, c)
                    act.dma_start(x_sb[:, :, :], xT[:, :, bass.ds(c * TB, TB)]).then_inc(s_x, 16)
                elif s == "store":
                    act.wait_ge(s_out, KH * c + KH)
                    act.dma_start(outT[:, :, bass.ds(c * TB, TB)], xres[:, :, :]).then_inc(s_store, 16)
                elif s in ("mean0", "mean1"):
                    l = int(s[-1])
                    act.wait_ge(s_xc[l], c + 1)
                    A(sq[:, :, :], (xn0, xn1)[l][:, :, :], ACT.Square).then_inc(s_sq[l], 1)
                elif s in ("var0", "var1"):
                    l = int(s[-1])
                    act.wait_ge(s_var[l], c + 1)
                    A(rstd[:, :], small[:, 1, :], ACT.Ln, bias=cst[:, K_EPS:K_EPS + 1]).then_inc(s_rstd[l], 1)
                    act.wait_ge(s_rstd[l], 2 * c + 1)
                    A(rstd[:, :], rstd[:, :], ACT.Exp, scale=-0.5).then_inc(s_rstd[l], 1)
                elif s == "updelta":
                    act.wait_ge(s_ud, c + 1)
                    after(act, s_acc0, c)
                    act.wait_ge(s_setup_dve, 5)
                    A(up[:, :], pair[0][:, 0, :], ACT.Copy).then_inc(s_uds, 1)
                    A(delta[:, :], pair[0][:, 1, :], ACT.Identity, bias=nlp[:, :]).then_inc(s_uds, 1)
                    A(keep[:, :], pair[0][:, 1, :], ACT.Abs, bias=nlp[:, :]).then_inc(s_uds, 1)
                elif s == "power":
                    act.wait_ge(s_pow, 9 * c + 7)
                    for g in range(MIN_ORDER):
                        A(q[:, g, :], q[:, g, :], ACT.Copy, scale=cm[:, g:g + 1]).then_inc(s_tay, 1)
                elif s == "experts":
                    act.wait_ge(s_lora, c + 1)
                    A(hw[:, :], pair[1][:, 0, :], ACT.Copy).then_inc(s_wt, 1)
                elif s == "gu":
                    act.wait_ge(s_gcl, NF * c + i + 1)
                    sigmoid(sig[:, i % 2, :], gcl[:, i % 2, :], s_sig, 3 * (NF * c + i))
                elif s == "winx":
                    act.wait_ge(s_winx, 4 * c + i + 1)
                    act.wait_ge(s_halo, c + 1)
                    A(xpad[:, 2 * i:2 * i + 2, KC - 1:], side[i % 2][:, :, :], ACT.Copy).then_inc(s_xpad, 1)
                elif s == "csilu":
                    for d in range(2):
                        j = 2 * i + d
                        act.wait_ge(s_conv, 40 * c + 10 * i + 9 + d)
                        if j >= 2:
                            act.wait_ge(s_u, NJ * c + j - 1)
                        sigmoid(cs[:, d, :], cv[:, j % 4, :], s_csig, 3 * (NJ * c + j))
                elif s == "wx":
                    act.wait_ge(s_ssm, c + 1)
                    A(ssm, small[:, 0, :], ACT.Copy).then_inc(s_ssq, 1)
                    A(sq[:, 0, :], small[:, 0, :], ACT.Square).then_inc(s_ssq, 1)
                elif s == "rms":
                    act.wait_ge(s_rms, c + 1)
                    A(rr, small[:, 1, :], ACT.Ln, bias=cst[:, K_EPS + 1:K_EPS + 2]).then_inc(s_rr, 1)
                    act.wait_ge(s_rr, 2 * c + 1)
                    A(rr, rr, ACT.Exp, scale=-0.5).then_inc(s_rr, 1)
                elif s == "bc":
                    n, which = bc_rows(i)
                    act.wait_ge(s_bc, NK * c + i + 1)
                    after(act, s_cmul if which else s_mul, NK * c)
                    A((Cb if which else Bb)[:, n:n + 2, :], pair[i % 2][:, :, :], ACT.Copy).then_inc(s_bce, 1)
                elif s == "dg_a":
                    act.wait_ge(s_dg, NJ * c + i + 1)
                    after(act, s_dt, NJ * c + i)
                    A(xb[:, :], side[i % 2][:, 0, :], ACT.Identity, bias=vec(V_BDT + i)).then_inc(s_xb, 1)
                    act.wait_ge(s_xb, NJ * c + i + 1)
                    A(ee[:, :], xb[:, :], ACT.Abs).then_inc(s_e, 1)
                    act.wait_ge(s_e, 2 * NJ * c + 2 * i + 1)
                    A(ee[:, :], ee[:, :], ACT.Exp, scale=-1.0).then_inc(s_e, 1)
                elif s == "dg_b":
                    act.wait_ge(s_gcg, NJ * c + i + 1)
                    after(act, s_gg, NJ * c + i)
                    sigmoid(gs[:, :], gg[:, i % 3, :], s_gsig, 3 * (NJ * c + i))
                elif s == "dg_c":
                    act.wait_ge(s_w, 2 * NJ * c + 2 * i + 2)
                    A(ww[:, :], ww[:, :], ACT.Ln).then_inc(s_ln, 1)
                elif s == "exp":
                    j, hn = i // 2, i % 2
                    act.wait_ge(s_dt, NJ * c + j + 1)
                    act.wait_ge(s_setup_dve, 6)
                    if hn == 0:
                        after(act, s_c0, NK * c + 2 * j - 2 if j > 1 else NK * c)
                        A(e0[:, j % 2, :], negA[:, j, :], ACT.Exp, scale=dt[:, j % 2, 0:1]).then_inc(s_e0, 1)
                    after(act, s_scan, NK * c + i - 1 if i > 1 else NK * c)
                    for n in range(NH):
                        m = A(dA[:, i % 2, n, 1:TB], dt[:, j % 2, 1:TB], ACT.Exp,
                              scale=negA[:, j, hn * NH + n:hn * NH + n + 1])
                    m.then_inc(s_exp, 1)
                elif s == "ffn1a":
                    act.wait_ge(s_ffn1a, c + 1)
                    A(ha[:, :], small[0:RX, 0, :], ACT.Copy, scale=LORA_SCALE).then_inc(s_ha, 1)

            run(act, step)

        @block.gpsimd
        def _(pool):
            TT = nc.gpsimd.tensor_tensor

            def step(s, i, c, _n):
                if s == "gu":
                    pool.wait_ge(s_sig, 3 * (NF * c + i) + 3)
                    TT(gcl[:, i % 2, :], gcl[:, i % 2, :], sig[:, i % 2, :], ALU.mult).then_inc(s_silu, 1)
                elif s == "csilu":
                    after(pool, s_z, NJ * c)
                    after(pool, s_wo, 4 * c)
                    for d in range(2):
                        j = 2 * i + d
                        pool.wait_ge(s_csig, 3 * (NJ * c + j) + 3)
                        TT(u[:, j, :], cv[:, j % 4, :], cs[:, d, :], ALU.mult).then_inc(s_u, 1)
                elif s == "dg_b":
                    pool.wait_ge(s_gsig, 3 * (NJ * c + i) + 3)
                    TT(gg[:, i % 3, :], gg[:, i % 3, :], gs[:, :], ALU.mult).then_inc(s_gg, 1)
                elif s == "dg_c":
                    pool.wait_ge(s_m, NJ * c + i + 1)
                    after(pool, s_exp, NK * c + 2 * i - 2 if i > 1 else NK * c)
                    TT(dt[:, i % 2, :], xb[:, :], ee[:, :], ALU.subtract).then_inc(s_dt, 1)
                    pool.wait_ge(s_dt, NJ * c + i + 1)
                    after(pool, s_mul, NK * c + 2 * i - 2 if i > 1 else NK * c)
                    TT(du[:, i % 2, :], dt[:, i % 2, :], u[:, i, :], ALU.mult).then_inc(s_du, 1)
                elif s == "cmul":
                    j, hn = i // 2, i % 2
                    pool.wait_ge(s_hprev, NK * c + i + 1)
                    pool.wait_ge(s_bce, NK * c + 8 * hn + 8)
                    TT(bs[:, i % 4, :, :], bs[:, i % 4, :, :], Cb[:, hn * NH:hn * NH + NH, :],
                       ALU.mult).then_inc(s_cmul, 1)

            run(pool, step)


_L0A, _L0F, _L1A, _L1F = "L0_attn_", "L0_ffn_", "L1_attn_", "L1_ffn_"


def kernel(**inputs):
    import numpy as np
    import concourse.bacc as _bacc
    from concourse.bass_utils import run_bass_kernel_spmd as _run

    a = {k: np.asarray(v) for k, v in inputs.items()}
    f32 = np.float32

    def rows(w, k):
        return w.reshape(k, P, -1).transpose(1, 0, 2).reshape(P, -1)

    def wide(w, f):
        out = np.zeros((w.shape[0], f), f32)
        out[:, :w.shape[1]] = w
        return out

    def col(v):
        return v.reshape(-1, P).T

    g, up = wide(a[_L0A + "ffn_gate_w"].T, F), wide(a[_L0A + "ffn_up_w"].T, F)
    down = wide(a[_L0A + "ffn_down_w"], F).T
    base, w1, wo = a[_L0F + "W_base"].T, a[_L1F + "w"].T, a[_L1A + "W_out"].T
    w_in = a[_L1A + "W_in"].T
    chunks = np.zeros((NCHUNK, P, CW), f32)
    chunks[UPG] = rows(np.concatenate([a[_L0A + "up_w"].T, a[_L0A + "gate_w"].T], 1), KH)
    for i in range(2):
        chunks[BASE + i] = rows(base[2 * P * i:2 * P * (i + 1)], 2)
        chunks[F1 + i] = rows(w1[2 * P * i:2 * P * (i + 1)], 2)
    for i in range(NF):
        chunks[GU + i] = rows(np.concatenate([g[:, P * i:P * (i + 1)], up[:, P * i:P * (i + 1)]], 1), KH)
    chunks[WXP] = rows(wide(a[_L1A + "W_x"].T, P), NJ)
    for i in range(4):
        chunks[WO + i] = rows(wo[2 * P * i:2 * P * (i + 1)], 2)
        chunks[WX + i] = rows(w_in[:, 2 * P * i:2 * P * (i + 1)], KH)
    down_w = down.reshape(NF, P, H)
    gate_w = np.stack([rows(w_in[:, DI + P * j:DI + P * (j + 1)], KH) for j in range(NJ)])

    res = np.zeros((P, NRES), f32)
    res[:, C_LORA_A:C_LORA_A + KH * P] = rows(a[_L0F + "lora_A"].transpose(1, 0, 2).reshape(H, P), KH)
    res[:, C_LORA_B:C_LORA_B + H] = a[_L0F + "lora_B"].reshape(P, H)
    res[:, C_LAO:C_LAO + H] = a[_L0A + "local_approx_output"].T
    res[:, C_FUSE:C_FUSE + G * H] = a[_L0A + "fuse_weight"].transpose(1, 2, 0).reshape(P, G * H)
    res[:, C_ROUTER:C_ROUTER + KH * E] = rows(a[_L0F + "W_router"].T, KH)
    res[:, C_ALOG:C_ALOG + NJ * NS] = rows(a[_L1A + "A_log"], NJ)
    res[:, C_LA1:C_LA1 + KH * RX] = rows(a[_L1F + "lora_a"], KH)
    v = res[:, C_VEC:]
    v[:, V_LP] = a[_L0A + "local_point"]
    v[:, V_B0:V_B0 + KH] = col(a[_L0F + "b_base"])
    v[:, V_CW:V_CW + NJ * KC] = rows(a[_L1A + "conv_w"], NJ)
    v[:, V_CB:V_CB + NJ] = col(a[_L1A + "conv_b"])
    v[:, V_BDT:V_BDT + NJ] = col(a[_L1A + "b_dt"])
    v[:, V_D:V_D + NJ] = col(a[_L1A + "D"])
    v[:, V_B1:V_B1 + KH] = col(a[_L1F + "b"])
    v[:, V_DISC:V_DISC + G] = a[_L0A + "discount_factor"]
    v[:, V_BR:V_BR + E] = a[_L0F + "b_router"]

    cst = np.zeros((P, NCONST), f32)
    cst[:, K_ID:K_ID + P] = np.eye(P)
    cst[:, K_MEAN:K_MEAN + P] = 1.0 / H
    for lo, n in ((0, RT), (RT, NS), (RT + NS, NS)):
        cst[lo:lo + n, K_RMS + lo:K_RMS + lo + n] = 1.0 / n
    cst[:, K_INV:K_INV + E] = 1.0 / np.arange(1, E + 1)
    cst[:, K_EPS], cst[:, K_EPS + 1] = 1e-5, 1e-6

    arrays = {
        "x_t": rows(a[_L0A + "hidden_states"][0].T, KH).reshape(P, KH, T), "chunks": chunks, "down_w": down_w,
        "gate_w": gate_w, "res": res, "wdt": a[_L1A + "W_dt"].T, "lb1": a[_L1F + "lora_b"], "consts": cst,
    }
    arrays = {k: np.ascontiguousarray(w) for k, w in arrays.items()}
    nc = _bacc.Bacc("TRN2", target_bir_lowering=False, num_devices=1)
    args = [nc.dram_tensor(k, w.shape, F32, kind="ExternalInput").ap() for k, w in arrays.items()]
    out = nc.dram_tensor("out_t", (P, KH, T), F32, kind="ExternalOutput").ap()
    build(nc, *args, out)
    r = _run(nc, [arrays], core_ids=[0])
    got = r.results[0]["out_t"]
    return got.transpose(2, 1, 0).reshape(1, T, H)
```

```python
from contextlib import ExitStack

import concourse.bass as bass
from concourse import mybir

F32 = mybir.dt.float32
F32R = mybir.dt.float32r
ALU = mybir.AluOpType
ACT = mybir.ActivationFunctionType
AX_X = mybir.AxisListType.X

P = 128
T = 1024
TB = 256
NB = T // TB
TC = TB // P
H = 512
KH = H // P
F = 1280
NF = F // P
G = 6
MIN_ORDER = 4
THD = 2.5
E, R0 = 8, 16
DI = 1024
NJ = DI // P
NS = 16
NH = NS // 2
NK = 2 * NJ
KC = 4
RT = 32
RX = 16
LORA_SCALE = 2.0
A_LOG_MAX = 80.0
SP_OPS = 10
FLOOR = -40.0

CW = 1024
UPG, BASE, GU, WXP, F1, WO, WX = 0, 1, 3, 13, 14, 16, 20
NCHUNK = 24
RING = 4

C_LORA_A, C_LORA_B, C_LAO, C_FUSE = 0, 512, 1024, 1536
C_ROUTER = C_FUSE + G * H
C_ALOG = C_ROUTER + KH * E
C_LA1 = C_ALOG + NJ * NS
C_VEC = C_LA1 + KH * RX
V_LP, V_B0, V_CW, V_CB, V_BDT, V_D, V_B1 = 0, 1, 5, 37, 45, 53, 61
V_DISC, V_BR = 65, 71
NRES = C_VEC + V_BR + E

K_ID, K_MEAN, K_RMS, K_INV, K_EPS, K_PICK = 0, 128, 256, 384, 392, 394
NCONST = K_PICK + 2 * NS


TENSOR_START = """
    mean0+ var0+ router+ updelta+ lora+ gu:0+ experts+ base+ gu:1+ gu:2+ down:0+ gu:3+ down:1+ down:2+ gu:4+
    gu:5+ gu:6+ down:3+ gu:7+ gu:8+ down:4+ down:5+ gu:9+ down:6+ down:7+ down:8+ down:9+ taylor+ loraout+
    mean1+ var1+ winx:0+ winx:1+ winx:2+ winx:3+ wx+ rms+ bc:0+ dg_a:0+ bc:1+ bc:2+ bc:3+
"""
TENSOR_BODY = """
    dg_a:1 wout:0- wout:1- wout:2- wout:3- ffn1a dg_a:2 ffn1 mean0+ red:0 dg_a:3 var0+ red:1 dg_a:4 router+
    updelta+ lora+ red:2 gu:0+ experts+ base+ red:3 gu:1+ gu:2+ down:0+ gu:3+ gu:4+ down:1+ gu:5+ down:2+
    dg_a:5 red:4 down:3+ dg_a:6 gu:6+ down:4+ red:5 down:5+ gu:7+ gu:8+ red:6 gu:9+ red:7 down:6+ down:7+
    dg_a:7 down:8+ down:9+ taylor+ loraout+ red:8 red:9 mean1+ var1+ winx:0+ winx:1+ winx:2+ winx:3+ red:10
    wx+ rms+ red:11 dg_a:0+ bc:0+ red:12 bc:1+ bc:2+ red:13 bc:3+ red:14 red:15
"""
VECTOR_START = """
    mean0+ var0+ router+ gu:0+ power+ experts+ gu:1+ gu:2+ hmul:0+ hmul:1+ hmul:2+ gu:3+ hmul:3+ gu:4+ gu:5+
    gu:6+ hmul:4+ hmul:5+ hmul:6+ gu:7+ gu:8+ gu:9+ hmul:7+ hmul:8+ hmul:9+ x1+ mean1+ var1+ conv:0+ conv:1+
    conv:2+ conv:3+ rms+ dg_a:0+ dg_b:0+ dg_c:0+ mul:0+
"""
VECTOR_BODY = """
    add0:0 scan:0 dg_b:1 save:0 mul:1 add0:1 dg_a:1 dg_c:1 scan:1 save:1 mul:2 fold:0 out- add0:2 scan:2
    save:2 dg_a:2 mul:3 add0:3 dg_b:2 fold:1 dg_c:2 keepx mean0+ scan:3 save:3 dg_a:3 mul:4 var0+ dg_b:3
    fold:2 router+ add0:4 fin:0 scan:4 power+ gu:0+ experts+ fold:3 dg_c:3 save:4 mul:5 gu:1+ fin:1 add0:5
    hmul:0+ scan:5 gu:2+ save:5 mul:6 hmul:1+ dg_b:4 gu:3+ add0:6 dg_a:4 scan:6 gu:4+ save:6 dg_c:4 hmul:2+
    hmul:3+ gu:5+ hmul:4+ fold:4 mul:7 dg_a:5 hmul:5+ dg_b:5 fold:5 dg_c:5 add0:7 scan:7 save:7 mul:8 fold:6
    add0:8 gu:6+ dg_b:6 scan:8 fold:7 save:8 mul:9 fin:2 add0:9 hmul:6+ gu:7+ gu:8+ scan:9 dg_a:6 save:9
    mul:10 add0:10 dg_c:6 hmul:7+ hmul:8+ gu:9+ scan:10 fold:8 save:10 hmul:9+ mul:11 add0:11 dg_b:7 fold:9
    fin:3 scan:11 dg_c:7 x1+ fold:10 mean1+ dg_a:7 save:11 mul:12 add0:12 scan:12 var1+ fold:11 fin:4 save:12
    mul:13 conv:0+ conv:1+ add0:13 conv:2+ conv:3+ scan:13 save:13 mul:14 add0:14 scan:14 save:14 rms+ mul:15
    fold:12 add0:15 fin:5 scan:15 save:15 dg_b:0+ fold:13 fold:14 dg_c:0+ fin:6 fold:15 dg_a:0+ mul:0+ fin:7
"""
SCALAR_START = """
    mean0+ var0+ updelta+ gu:0+ power+ experts+ gu:1+ gu:2+ gu:3+ gu:4+ gu:5+ gu:6+ gu:7+ gu:8+ gu:9+ mean1+
    var1+ winx:0+ winx:1+ csilu:0+ winx:2+ csilu:1+ winx:3+ csilu:2+ csilu:3+ wx+ rms+ bc:0+ dg_a:0+ bc:1+
    bc:2+ dg_c:0+ bc:3+ dg_b:0+ exp:0+
"""
SCALAR_BODY = """
    dg_a:1 xload+ exp:1 dg_c:1 exp:2 store- exp:3 dg_a:2 dg_b:1 ffn1a dg_c:2 mean0+ skip:0 dg_a:3 var0+ skip:1
    exp:4 updelta+ gu:0+ power+ experts+ skip:2 dg_c:3 dg_b:2 exp:5 gu:1+ dg_a:4 exp:6 gu:2+ dg_c:4 gu:3+
    dg_b:3 gu:4+ skip:3 exp:7 gu:5+ dg_a:5 dg_c:5 exp:8 dg_a:6 dg_b:4 skip:4 exp:9 dg_c:6 gu:6+ gu:7+ gu:8+
    exp:10 gu:9+ exp:11 skip:5 dg_a:7 exp:12 dg_c:7 dg_b:5 exp:13 mean1+ skip:6 skip:7 dg_b:6 var1+ exp:14
    winx:0+ winx:1+ csilu:0+ winx:2+ csilu:1+ winx:3+ csilu:2+ csilu:3+ wx+ rms+ dg_b:7 exp:15 bc:0+ dg_a:0+
    bc:1+ bc:2+ dg_c:0+ bc:3+ exp:0+ dg_b:0+
"""
GPSIMD_START = """
    gu:0+ gu:1+ gu:2+ gu:3+ gu:4+ gu:5+ gu:6+ gu:7+ gu:8+ gu:9+ csilu:0+ csilu:1+ csilu:2+ csilu:3+ dg_c:0+
    dg_b:0+
"""
GPSIMD_BODY = """
    cmul:0 dg_c:1 cmul:1 cmul:2 dg_c:2 dg_b:1 cmul:3 dg_b:2 dg_c:3 gu:0+ gu:1+ cmul:4 cmul:5 gu:2+ gu:3+
    dg_c:4 gu:4+ cmul:6 gu:5+ dg_c:5 dg_b:3 cmul:7 dg_b:4 gu:6+ gu:7+ gu:8+ cmul:8 gu:9+ dg_c:6 cmul:9 cmul:10
    dg_b:5 cmul:11 dg_c:7 cmul:12 csilu:0+ csilu:1+ csilu:2+ csilu:3+ dg_b:6 cmul:13 cmul:14 dg_b:7 cmul:15
    dg_c:0+ dg_b:0+
"""


def steps(text):
    out = []
    for word in text.split():
        name, _, i = word.rstrip("+-").partition(":")
        out.append(({"+": 1, "-": -1}.get(word[-1], 0), name, int(i or 0)))
    return out


def streamed(order):
    out = []
    for d, s, i in order:
        if s in ("updelta", "wx"):
            out.append(({"updelta": UPG, "wx": WXP}[s], 0, d))
        elif s in ("base", "ffn1"):
            out += [({"base": BASE, "ffn1": F1}[s], kk, d) for kk in range(2)]
        elif s in ("gu", "wout", "winx"):
            out.append(({"gu": GU, "wout": WO, "winx": WX}[s], i, d))
        elif s in ("down", "dg_a"):
            out.append((s, i, d))
    return out


def in_ring(order):
    return [c for c in streamed(order) if c[0] not in ("down", "dg_a")]


class Orders:
    def __init__(self, start, body):
        self.start = steps(start)
        self.body = steps(body)
        self.first = [s for s in self.body if s[0] >= 0]
        self.last = [s for s in self.body if s[0] <= 0] + [(0,) + s[1:] for s in self.body if s[0] < 0]


def run(eng, orders, stretch):
    stretch(orders.start, 0, -1, 0)
    stretch(orders.first, N0, 0, 0)
    with eng.Fori(1, NB - 1) as b:
        stretch(orders.body, N0 + N1, b, b - 1)
    stretch(orders.last, N0 + N1 + N2 * (NB - 2), NB - 1, 0)


def stepper(step):
    def stretch(order, first, b, turns):
        for d, s, i in order:
            step(s, i, b + d, (first, turns))
            first += len(in_ring([(d, s, i)]))
    return stretch


TENSOR, VECTOR = Orders(TENSOR_START, TENSOR_BODY), Orders(VECTOR_START, VECTOR_BODY)
SCALAR, GPSIMD = Orders(SCALAR_START, SCALAR_BODY), Orders(GPSIMD_START, GPSIMD_BODY)
N0, N1, N2 = len(in_ring(TENSOR.start)), len(in_ring(TENSOR.first)), len(in_ring(TENSOR.body))
assert N2 % RING == 0


def bc_rows(i):
    part, r = i // 4, 2 * (i % 4)
    return (part // 2) * NH + r, part % 2


def after(eng, sem, n):
    if not isinstance(n, int) or n > 0:
        eng.wait_ge(sem, n)


def build(nc, xT, chunks, down_w, gate_w, res, lb1, consts, outT):
    with ExitStack() as ctx:
        def sb(name, shape, dtype=F32):
            return ctx.enter_context(nc.sbuf_tensor(name, shape, dtype))

        def bank(name, shape=(P, 2, TB)):
            return ctx.enter_context(nc.psum_tensor(name, list(shape), F32))

        def sem(name):
            return ctx.enter_context(nc.semaphore(name))

        ring = sb("ring", [P, RING, CW])
        resw = sb("resw", [P, NRES])
        down_sb = sb("down_sb", [P, 2, H])
        gate_sb = sb("gate_sb", [P, 2, H + P])
        lb1_sb = sb("lb1_sb", [RX, H])
        cst = sb("cst", [P, NCONST])
        negA = sb("negA", [P, NJ, NS])
        cm = sb("cm", [P, G])
        nlp = sb("nlp", [P, 1])
        ones8 = sb("ones8", [P, E])
        cum = sb("cum", [P, TC, E])
        x_in = sb("x_in", [P, KH, TB])
        x_sb = sb("x_sb", [P, KH, TB])
        xn0 = sb("xn0", [P, KH, TB])
        sq = sb("sq", [P, KH, TB])
        rstd = sb("rstd", [P, TB])
        up = sb("up", [P, TB])
        delta = sb("delta", [P, TB])
        keep = sb("keep", [P, TB])
        q = sb("q", [P, G, TB])
        z8 = sb("z8", [P, TC, E])
        zs = sb("zs", [P, TC, E])
        tau = sb("tau", [P, TC])
        hw = sb("hw", [P, TB])
        gcl = sb("gcl", [P, 3, TB])
        sig = sb("sig", [P, 3, TB])
        h = sb("h", [P, 3, TB])
        xres = sb("xres", [P, KH, TB])
        xn1 = sb("xn1", [P, KH, TB])
        xpad = sb("xpad", [P, 4, TB + KC - 1])
        halo = sb("halo", [P, NJ, KC - 1])
        u = sb("u", [P, NJ, TB])
        z = sb("z", [P, NJ, TB])
        bct = sb("bct", [P, TB])
        bcr = sb("bcr", [P, TB], F32R)
        pick = sb("pick", [P, 2 * NS], F32R)
        Bb = sb("Bb", [P, NS, TB])
        Cb = sb("Cb", [P, NS, TB])
        xb = sb("xb", [P, TB])
        ee = sb("ee", [P, TB])
        ww = sb("ww", [P, TB])
        gs = sb("gs", [P, TB])
        gg = sb("gg", [P, 4, TB])
        dt = sb("dt", [P, 2, TB])
        du = sb("du", [P, 2, TB])
        e0 = sb("e0", [P, 2, NS])
        c0 = sb("c0", [P, 2, NH])
        hprev = sb("hprev", [P, NJ, NS])
        dA = sb("dA", [P, 2, NH, TB])
        bs = sb("bs", [P, 4, NH, TB])

        wrep = sig[:, 2, :].rearrange("p (a b) -> p a b", a=TC)
        cv, cs = q[:, 0:4, :], sig
        ssm, rr = h[:, 0, :], h[:, 1, :]
        ha = hw[0:RX, :]

        def vec(i, rows=P):
            return resw[0:rows, C_VEC + i:C_VEC + i + 1]

        ident = cst[:, K_ID:K_ID + P]
        mean_w = cst[:, K_MEAN:K_MEAN + P]
        rms_w = cst[:, K_RMS:K_RMS + P]
        inv_k = cst[:, K_INV:K_INV + E]
        lora_a = resw[:, C_LORA_A:C_LORA_A + KH * P].rearrange("p (k m) -> p k m", k=KH)
        lora_b = resw[:, C_LORA_B:C_LORA_B + H]
        lao = resw[:, C_LAO:C_LAO + H]
        fuse = resw[:, C_FUSE:C_FUSE + G * H].rearrange("p (g m) -> p g m", g=G)
        router = resw[:, C_ROUTER:C_ROUTER + KH * E].rearrange("p (k m) -> p k m", k=KH)
        a_log = resw[:, C_ALOG:C_ALOG + NJ * NS]
        la1 = resw[:, C_LA1:C_LA1 + KH * RX].rearrange("p (k m) -> p k m", k=KH)
        disc = resw[:, C_VEC + V_DISC:C_VEC + V_DISC + G]
        b_router = resw[:, C_VEC + V_BR:C_VEC + V_BR + E]

        pair = [bank("pair0"), bank("pair1"), bank("pair2")]
        acc = [bank("acc0"), bank("acc1")]
        ybank = bank("ybank")
        small = bank("small")
        side = bank("side")

        s_res, s_setup_act, s_setup_dve = sem("s_res"), sem("s_setup_act"), sem("s_setup_dve")
        s_chunk = [sem(f"s_chunk{i}") for i in range(RING)]
        s_downw = [sem("s_downw0"), sem("s_downw1")]
        s_gatew = [sem("s_gatew0"), sem("s_gatew1")]
        s_basew, s_f1w, s_wo = sem("s_basew"), sem("s_f1w"), sem("s_wo")
        s_x = sem("s_x")
        s_mean = [sem("s_mean0"), sem("s_mean1")]
        s_xc = [sem("s_xc0"), sem("s_xc1")]
        s_sq = [sem("s_sq0"), sem("s_sq1")]
        s_var = [sem("s_var0"), sem("s_var1")]
        s_rstd = [sem("s_rstd0"), sem("s_rstd1")]
        s_xn = [sem("s_xn0"), sem("s_xn1")]
        s_router, s_sparse = sem("s_router"), sem("s_sparse")
        s_ud, s_uds, s_pow, s_tay = sem("s_ud"), sem("s_uds"), sem("s_pow"), sem("s_tay")
        s_lora, s_wt, s_hw = sem("s_lora"), sem("s_wt"), sem("s_hw")
        s_gu, s_gcl, s_sig, s_silu, s_h, s_down = (sem("s_gu"), sem("s_gcl"), sem("s_sig"), sem("s_silu"),
                                                  sem("s_h"), sem("s_down"))
        s_acc0, s_x1, s_keepx = sem("s_acc0"), sem("s_x1"), sem("s_keepx")
        s_winx, s_xpad, s_conv, s_csig, s_u, s_halo = (sem("s_winx"), sem("s_xpad"), sem("s_conv"), sem("s_csig"),
                                                       sem("s_u"), sem("s_halo"))
        s_ssm, s_ssq, s_rms, s_rr, s_bct = sem("s_ssm"), sem("s_ssq"), sem("s_rms"), sem("s_rr"), sem("s_bct")
        s_pick, s_bc, s_bce = sem("s_pick"), sem("s_bc"), sem("s_bce")
        s_dg, s_xb, s_gcg, s_e, s_w, s_ln, s_m = (sem("s_dg"), sem("s_xb"), sem("s_gcg"), sem("s_e"), sem("s_w"),
                                                  sem("s_ln"), sem("s_m"))
        s_dt, s_du, s_gsig, s_gg = sem("s_dt"), sem("s_du"), sem("s_gsig"), sem("s_gg")
        s_e0, s_exp, s_c0, s_mul, s_add0, s_scan, s_hprev, s_cmul, s_fold, s_skip, s_red, s_fa, s_z = (
            sem("s_e0"), sem("s_exp"), sem("s_c0"), sem("s_mul"), sem("s_add0"), sem("s_scan"), sem("s_hprev"),
            sem("s_cmul"), sem("s_fold"), sem("s_skip"), sem("s_red"), sem("s_fa"), sem("s_z"))
        s_ffn1a, s_ha, s_ffn1, s_out, s_store = (sem("s_ffn1a"), sem("s_ha"), sem("s_ffn1"), sem("s_out"),
                                                 sem("s_store"))
        NRESDMA = 3

        block = ctx.enter_context(nc.Block())

        @block.sync
        def _(sp):
            def ring_used(kind, i, c):
                sem_, n = {UPG: (s_ud, c + 1), BASE: (s_basew, 2 * c + i + 1), GU: (s_gu, NF * c + i + 1),
                           WXP: (s_ssm, c + 1), F1: (s_f1w, 2 * c + i + 1), WO: (s_wo, 4 * c + i + 1),
                           WX: (s_winx, 4 * c + i + 1)}[kind]
                sp.wait_ge(sem_, n)

            def loads(order, first, b, before):
                ahead = list(before)
                for kind, i, d in streamed(order):
                    c = b + d
                    if kind == "down":
                        after(sp, s_down, NF * c + i - 1)
                        sp.dma_start(down_sb[:, i % 2, :], down_w[i]).then_inc(s_downw[i % 2], 16)
                    elif kind == "dg_a":
                        after(sp, s_dg, NJ * c + i - 1)
                        sp.dma_start(gate_sb[:, i % 2, :], gate_w[i]).then_inc(s_gatew[i % 2], 16)
                    else:
                        if len(ahead) >= RING:
                            ring_used(*ahead[-RING])
                        slot = first % RING
                        sp.dma_start(ring[:, slot, :], chunks[kind + i]).then_inc(s_chunk[slot], 16)
                        ahead.append((kind, i, c))
                        first += 1

            def stretch(order, first, b, _turns):
                before = {id(TENSOR.start): [], id(TENSOR.first): TENSOR.start}.get(id(order), TENSOR.body)
                loads(order, first, b, [(kind, i, b - 1 + d) for kind, i, d in in_ring(before)][-RING:])

            sp.dma_start(x_in[:, :, :], xT[:, :, 0:TB]).then_inc(s_x, 16)
            sp.dma_start(cst[:, :], consts).then_inc(s_res, 16)
            sp.dma_start(resw[:, :], res).then_inc(s_res, 16)
            sp.dma_start(lb1_sb[:, :], lb1).then_inc(s_res, 16)
            run(sp, TENSOR, stretch)
            sp.wait_ge(s_store, 16 * NB)

        @block.tensor
        def _(pe):
            pe.wait_ge(s_res, 16 * NRESDMA)
            def chunk(n, more=0):
                at = n[0] + more
                pe.wait_ge(s_chunk[at % RING], 16 * (at // RING + 1) + 16 * (N2 // RING) * n[1])
                return ring[:, at % RING, :]

            def mm(out, w, x, start, stop):
                return nc.tensor.matmul(out, w, x, start=start, stop=stop, skip_group_check=True)

            def norm_sum(l, c, out, src):
                for k in range(KH):
                    m = mm(out, mean_w, src[:, k, :], k == 0, k == KH - 1)
                return m

            def step(s, i, c, t):
                if s in ("mean0", "mean1"):
                    l = int(s[-1])
                    src = (x_in, x_sb)[l]
                    if l == 0:
                        pe.wait_ge(s_x, 16 * c + 16)
                        after(pe, s_ha, c)
                    else:
                        pe.wait_ge(s_x1, KH * c + KH)
                    norm_sum(l, c, small[:, 0, :], src).then_inc(s_mean[l], 1)
                elif s in ("var0", "var1"):
                    l = int(s[-1])
                    pe.wait_ge(s_sq[l], c + 1)
                    norm_sum(l, c, small[:, 1, :], sq).then_inc(s_var[l], 1)
                elif s == "router":
                    pe.wait_ge(s_xn[0], c + 1)
                    for tc in range(TC):
                        for k in range(KH):
                            m = mm(small[:, 0, tc * E:(tc + 1) * E], xn0[:, k, tc * P:(tc + 1) * P],
                                   router[:, k, :], k == 0, k == KH - 1)
                    m.then_inc(s_router, 1)
                elif s == "updelta":
                    after(pe, s_bce, NK * c)
                    w = chunk(t).rearrange("p (k m) -> p k m", k=KH)
                    for half in range(2):
                        for k in range(KH):
                            m = mm(pair[0][:, half, :], w[:, k, half * P:(half + 1) * P], xn0[:, k, :],
                                   k == 0, k == KH - 1)
                    m.then_inc(s_ud, 1)
                elif s == "lora":
                    for k in range(KH):
                        m = mm(pair[1][:, 1, :], lora_a[:, k, :], xn0[:, k, :], k == 0, k == KH - 1)
                elif s == "experts":
                    pe.wait_ge(s_sparse, SP_OPS * c + SP_OPS)
                    for tc in range(TC):
                        m = nc.tensor.matmul(pair[1][:, 0, tc * P:(tc + 1) * P], wrep[:, tc, :], ident,
                                             start=True, stop=True, is_transpose=True, skip_group_check=True)
                    m.then_inc(s_lora, 1)
                elif s == "gu":
                    if i == 0:
                        pe.wait_ge(s_uds, 3 * c + 3)
                    elif i == 1:
                        pe.wait_ge(s_hw, c + 1)
                    else:
                        after(pe, s_h, NF * c + i - 2 if i > 2 else NF * c)
                    w = chunk(t).rearrange("p (k m) -> p k m", k=KH)
                    for half in range(2):
                        for k in range(KH):
                            m = mm(pair[i % 3][:, half, :], w[:, k, half * P:(half + 1) * P], xn0[:, k, :],
                                   k == 0, k == KH - 1)
                    m.then_inc(s_gu, 1)
                elif s == "base":
                    after(pe, s_keepx, KH * c)
                    for kk in range(2):
                        w = chunk(t, kk).rearrange("p (k m) -> p k m", k=2)
                        for k in range(2):
                            for mt in range(KH):
                                m = mm(acc[mt // 2][:, mt % 2, :], w[:, k, mt * P:(mt + 1) * P],
                                       xn0[:, 2 * kk + k, :], kk == 0 and k == 0 and mt % 2 == 0, False)
                        m.then_inc(s_basew, 1)
                elif s == "down":
                    pe.wait_ge(s_h, NF * c + i + 1)
                    pe.wait_ge(s_downw[i % 2], 16 * (NF // 2) * c + 16 * (i // 2 + 1))
                    for mt in range(KH):
                        m = mm(acc[mt // 2][:, mt % 2, :], down_sb[:, i % 2, mt * P:(mt + 1) * P], h[:, i % 3, :],
                               False, False)
                    m.then_inc(s_down, 1)
                elif s == "taylor":
                    for mt in range(KH):
                        m = mm(acc[mt // 2][:, mt % 2, :], lao[:, mt * P:(mt + 1) * P], up[:, :], False, False)
                    pe.wait_ge(s_tay, 4 * c + 4)
                    pe.wait_ge(s_pow, 9 * c + 9)
                    for g in range(G):
                        for mt in range(KH):
                            m = mm(acc[mt // 2][:, mt % 2, :], fuse[:, g, mt * P:(mt + 1) * P], q[:, g, :],
                                   False, False)
                elif s == "loraout":
                    pe.wait_ge(s_hw, c + 1)
                    for mt in range(KH):
                        m = mm(acc[mt // 2][:, mt % 2, :], lora_b[:, mt * P:(mt + 1) * P], hw[:, :],
                               False, True)
                    m.then_inc(s_acc0, 1)
                elif s == "winx":
                    pe.wait_ge(s_xn[1], c + 1)
                    if i >= 2:
                        pe.wait_ge(s_xpad, 4 * c + i - 1)
                    else:
                        pe.wait_ge(s_h, NF * c + NF)
                    w = chunk(t).rearrange("p (k m) -> p k m", k=KH)
                    for half in range(2):
                        for k in range(KH):
                            m = mm(pair[i % 2][:, half, :], w[:, k, half * P:(half + 1) * P], xn1[:, k, :],
                                   k == 0, k == KH - 1)
                    m.then_inc(s_winx, 1)
                elif s == "wx":
                    w_x = chunk(t).rearrange("p (k m) -> p k m", k=NJ)
                    for k in range(NJ):
                        pe.wait_ge(s_u, NJ * c + k + 1)
                        m = mm(small[:, 0, :], w_x[:, k, :], u[:, k, :], k == 0, k == NJ - 1)
                    m.then_inc(s_ssm, 1)
                elif s == "rms":
                    pe.wait_ge(s_ssq, 2 * c + 2)
                    mm(small[:, 1, :], rms_w, sq[:, 0, :], True, True).then_inc(s_rms, 1)
                elif s == "bc":
                    for r in range(4 * i, 4 * i + 4):
                        if r < 2:
                            pe.wait_ge(s_bct, 3 * c + 3)
                            pe.wait_ge(s_xpad, 4 * c + 4)
                            pe.wait_ge(s_pick, 1)
                        else:
                            pe.wait_ge(s_bce, NK * c + r - 1)
                        for half in range(2):
                            n, which = bc_rows(r)
                            row = NS * which + n + half
                            m = mm(pair[r % 2][:, half, :],
                                   pick[:, row:row + 1].to_broadcast([P, P]), bcr[:, :], True, True)
                        m.then_inc(s_bc, 1)
                elif s == "dg_a":
                    pe.wait_ge(s_bct, 3 * c + 1)
                    after(pe, s_gcg, NJ * c + i)
                    after(pe, s_xb, NJ * c + i)
                    pe.wait_ge(s_gatew[i % 2], 16 * (NJ // 2) * c + 16 * (i // 2 + 1))
                    mm(side[:, 0, :], gate_sb[0:RT, i % 2, H:H + P], bct[0:RT, :], True, True)
                    for k in range(KH):
                        m = mm(side[:, 1, :], gate_sb[:, i % 2, k * P:(k + 1) * P], xn1[:, k, :],
                               k == 0, k == KH - 1)
                    m.then_inc(s_dg, 1)
                elif s == "red":
                    j, hn = i // 2, i % 2
                    pe.wait_ge(s_fold, 2 * NK * c + 2 * i + 2)
                    if hn == 0:
                        after(pe, s_fa, NJ * c + j)
                    for n in range(NH // 4):
                        m = mm(ybank[:, 0, :], ident, bs[:, i % 4, n, :], hn == 0 and n == 0,
                               hn == 1 and n == NH // 4 - 1)
                    m.then_inc(s_red, 1)
                elif s == "ffn1a":
                    for k in range(KH):
                        m = mm(small[0:RX, 0, :], la1[:, k, :], xn1[:, k, :], k == 0, k == KH - 1)
                    m.then_inc(s_ffn1a, 1)
                elif s == "ffn1":
                    after(pe, s_out, KH * c)
                    for kk in range(2):
                        w = chunk(t, kk).rearrange("p (k m) -> p k m", k=2)
                        for k in range(2):
                            for mt in range(KH):
                                m = mm(acc[mt // 2][:, mt % 2, :], w[:, k, mt * P:(mt + 1) * P],
                                       xn1[:, 2 * kk + k, :], kk == 0 and k == 0 and mt % 2 == 0, False)
                        m.then_inc(s_f1w, 1)
                    pe.wait_ge(s_ha, c + 1)
                    for mt in range(KH):
                        m = mm(acc[mt // 2][:, mt % 2, :], lb1_sb[:, mt * P:(mt + 1) * P], ha, False, True)
                    m.then_inc(s_ffn1, 1)
                elif s == "wout":
                    if isinstance(c, int) and c == NB - 1:
                        pe.wait_ge(s_keepx, KH * c + KH)
                    else:
                        pe.wait_ge(s_x1, KH * c + 2 * KH)
                    pe.wait_ge(s_z, NJ * c + 2 * i + 2)
                    w = chunk(t).rearrange("p (k m) -> p k m", k=2)
                    for k in range(2):
                        for mt in range(KH):
                            m = mm(acc[mt // 2][:, mt % 2, :], w[:, k, mt * P:(mt + 1) * P], z[:, 2 * i + k, :],
                                   i == 0 and k == 0 and mt % 2 == 0, i == 3 and k == 1)
                    m.then_inc(s_wo, 1)

            run(pe, TENSOR, stepper(step))

        @block.vector
        def _(dve):
            V = nc.vector
            V.memset(hprev[:, :, :], 0.0).then_inc(s_setup_dve, 1)
            V.memset(dA[:, :, :, 0:1], 0.0).then_inc(s_setup_dve, 1)
            V.memset(ones8[:, :], 1.0).then_inc(s_setup_dve, 1)
            V.memset(halo[:, :, :], 0.0).then_inc(s_halo, 1)
            dve.wait_ge(s_res, 16 * NRESDMA)
            V.tensor_scalar(negA[:, :, :].rearrange("p j n -> p (j n)"), a_log, A_LOG_MAX, None,
                            ALU.min).then_inc(s_setup_dve, 1)
            V.tensor_scalar(nlp[:, :], vec(V_LP), -1.0, None, ALU.mult).then_inc(s_setup_dve, 1)
            V.tensor_copy(pick[:, :], cst[:, K_PICK:K_PICK + 2 * NS]).then_inc(s_pick, 1)
            dve.wait_ge(s_setup_act, 2)
            V.tensor_scalar(negA[:, :, :], negA[:, :, :], -1.0, None, ALU.mult).then_inc(s_setup_dve, 1)

            def step(s, i, c, _n):
                if s in ("mean0", "mean1"):
                    l = int(s[-1])
                    xn = (xn0, xn1)[l]
                    dve.wait_ge(s_mean[l], c + 1)
                    if l == 1:
                        after(dve, s_dg, NJ * c)
                        after(dve, s_ffn1, c)
                    V.tensor_tensor(xn[:, :, :], (x_in, x_sb)[l][:, :, :],
                                    small[:, 0, :].unsqueeze(1).to_broadcast([P, KH, TB]),
                                    ALU.subtract).then_inc(s_xc[l], 1)
                elif s in ("var0", "var1"):
                    l = int(s[-1])
                    xn = (xn0, xn1)[l]
                    dve.wait_ge(s_rstd[l], 2 * c + 2)
                    V.tensor_tensor(xn[:, :, :], xn[:, :, :], rstd[:, :].unsqueeze(1).to_broadcast([P, KH, TB]),
                                    ALU.mult).then_inc(s_xn[l], 1)
                elif s == "router":
                    dve.wait_ge(s_router, c + 1)
                    at = SP_OPS * c
                    V.tensor_tensor(z8[:, :, :], small[:, 0, 0:TC * E].rearrange("p (a b) -> p a b", a=TC),
                                    b_router.unsqueeze(1).to_broadcast([P, TC, E]), ALU.add).then_inc(s_sparse, 1)
                    dve.wait_ge(s_sparse, at + 1)
                    V.tensor_copy(cum[:, :, :], z8[:, :, :])
                    for tc in range(TC):
                        V.max(zs[:, tc, :], z8[:, tc, :]).then_inc(s_sparse, 1)
                    for tc in range(TC):
                        dve.wait_ge(s_sparse, at + 2 + tc)
                        V.tensor_tensor_scan(cum[:, tc, :], ones8[:, :], zs[:, tc, :], 0.0, ALU.mult,
                                             ALU.add).then_inc(s_sparse, 1)
                    dve.wait_ge(s_sparse, at + 5)
                    V.scalar_tensor_tensor(zs[:, :, :], cum[:, :, :], -1.0,
                                           inv_k.unsqueeze(1).to_broadcast([P, TC, E]), ALU.add,
                                           ALU.mult).then_inc(s_sparse, 1)
                    dve.wait_ge(s_sparse, at + 6)
                    V.tensor_reduce(tau[:, :], zs[:, :, :], AX_X, ALU.max).then_inc(s_sparse, 1)
                    dve.wait_ge(s_sparse, at + 7)
                    for tc in range(TC):
                        V.tensor_scalar(z8[:, tc, :], z8[:, tc, :], tau[:, tc:tc + 1], 0.0, ALU.subtract,
                                        ALU.max).then_inc(s_sparse, 1)
                    dve.wait_ge(s_sparse, at + 9)
                    V.tensor_copy(wrep[:, :, :].rearrange("p a (e r) -> p a e r", e=E),
                                  z8[:, :, :].unsqueeze(3).to_broadcast([P, TC, E, R0])).then_inc(s_sparse, 1)
                elif s == "power":
                    dve.wait_ge(s_uds, 3 * c + 3)
                    V.tensor_scalar(keep[:, :], keep[:, :], THD, None, ALU.is_le).then_inc(s_pow, 1)
                    for g in range(G):
                        if g:
                            dve.wait_ge(s_pow, 9 * c + g + 1)
                        V.tensor_tensor(q[:, g, :], q[:, g - 1, :] if g else up[:, :], delta[:, :],
                                        ALU.mult).then_inc(s_pow, 1)
                    for n, g in enumerate(range(MIN_ORDER, G)):
                        dve.wait_ge(s_pow, 9 * c + 7)
                        V.scalar_tensor_tensor(q[:, g, :], q[:, g, :], cm[:, g:g + 1], keep[:, :], ALU.mult,
                                               ALU.mult).then_inc(s_pow, 1)
                elif s == "experts":
                    dve.wait_ge(s_wt, c + 1)
                    V.tensor_tensor(hw[:, :], pair[1][:, 1, :], hw[:, :], ALU.mult).then_inc(s_hw, 1)
                elif s == "gu":
                    dve.wait_ge(s_gu, NF * c + i + 1)
                    after(dve, s_h, NF * c + i - 2 if i > 2 else NF * c)
                    V.tensor_scalar(gcl[:, i % 3, :], pair[i % 3][:, 0, :], FLOOR, None, ALU.max).then_inc(s_gcl, 1)
                elif s == "hmul":
                    dve.wait_ge(s_silu, NF * c + i + 1)
                    after(dve, s_down, NF * c + i - 2 if i > 2 else NF * c)
                    V.tensor_tensor(h[:, i % 3, :], gcl[:, i % 3, :], pair[i % 3][:, 1, :],
                                    ALU.mult).then_inc(s_h, 1)
                elif s == "x1":
                    dve.wait_ge(s_acc0, c + 1)
                    after(dve, s_keepx, KH * c)
                    for mt in range(KH):
                        V.scalar_tensor_tensor(x_sb[:, mt, :], acc[mt // 2][:, mt % 2, :], vec(V_B0 + mt),
                                               x_in[:, mt, :], ALU.add, ALU.add).then_inc(s_x1, 1)
                elif s == "conv":
                    dve.wait_ge(s_xpad, 4 * c + i + 1)
                    xp, hl = xpad[:, 2 * (i % 2):2 * (i % 2) + 2, :], halo[:, 2 * i:2 * i + 2, :]
                    dve.wait_ge(s_halo, 8 * c + 2 * i + 1)
                    V.tensor_copy(xp[:, :, 0:KC - 1], hl).then_inc(s_halo, 1)
                    dve.wait_ge(s_halo, 8 * c + 2 * i + 2)
                    V.tensor_copy(hl, xp[:, :, TB:TB + KC - 1]).then_inc(s_halo, 1)
                    after(dve, s_u, NJ * c + 2 * i - 2 if i > 1 else NJ * c)
                    for tap in range(KC + 1):
                        for d in range(2):
                            j = 2 * i + d
                            acc_ = cv[:, j % 4, :]
                            if tap:
                                dve.wait_ge(s_conv, 40 * c + 10 * i + 2 * tap - 1 + d)
                            if tap == 0:
                                V.tensor_scalar(acc_, xp[:, d, 0:TB], vec(V_CW + KC * j), vec(V_CB + j), ALU.mult,
                                                ALU.add).then_inc(s_conv, 1)
                            elif tap < KC:
                                V.scalar_tensor_tensor(acc_, xp[:, d, tap:tap + TB], vec(V_CW + KC * j + tap),
                                                       acc_, ALU.mult, ALU.add).then_inc(s_conv, 1)
                            else:
                                V.tensor_scalar(acc_, acc_, FLOOR, None, ALU.max).then_inc(s_conv, 1)
                elif s == "rms":
                    dve.wait_ge(s_rr, 2 * c + 2)
                    V.tensor_tensor(bct[:, :], ssm, rr, ALU.mult).then_inc(s_bct, 1)
                    dve.wait_ge(s_bct, 3 * c + 1)
                    V.tensor_copy(bcr[:, :], bct[:, :]).then_inc(s_bct, 1)
                    dve.wait_ge(s_bct, 3 * c + 2)
                    V.tensor_tensor(bcr[P // 2:, :], bct[P // 2:, :], bcr[P // 2:, :].bitcast(F32),
                                    ALU.subtract).then_inc(s_bct, 1)
                elif s == "keepx":
                    dve.wait_ge(s_ffn1, c + 1)
                    after(dve, s_out, KH * c)
                    for mt in range(KH):
                        V.scalar_tensor_tensor(xres[:, mt, :], acc[mt // 2][:, mt % 2, :], vec(V_B1 + mt),
                                               x_sb[:, mt, :], ALU.add, ALU.add).then_inc(s_keepx, 1)
                elif s == "dg_a":
                    dve.wait_ge(s_dg, NJ * c + i + 1)
                    dve.wait_ge(s_xb, NJ * c + i + 1)
                    after(dve, s_z, NJ * c + i - 3)
                    V.tensor_scalar(gg[:, i % 4, :], side[:, 1, :], FLOOR, None, ALU.max).then_inc(s_gcg, 1)
                elif s == "dg_b":
                    dve.wait_ge(s_e, 2 * NJ * c + 2 * i + 2)
                    after(dve, s_m, NJ * c + i)
                    V.tensor_scalar(ww[:, :], ee[:, :], 1.0, None, ALU.add).then_inc(s_w, 1)
                    dve.wait_ge(s_w, 2 * NJ * c + 2 * i + 1)
                    V.scalar_tensor_tensor(ee[:, :], ww[:, :], -1.0, ee[:, :], ALU.add,
                                           ALU.subtract).then_inc(s_w, 1)
                elif s == "dg_c":
                    dve.wait_ge(s_ln, NJ * c + i + 1)
                    V.scalar_tensor_tensor(xb[:, :], xb[:, :], 0.0, ww[:, :], ALU.max, ALU.add).then_inc(s_m, 1)
                elif s == "mul":
                    j, hn = i // 2, i % 2
                    dve.wait_ge(s_du, NJ * c + j + 1)
                    dve.wait_ge(s_bce, NK * c + 8 * hn + 4)
                    after(dve, s_red, NK * c + i - 3)
                    V.tensor_tensor(bs[:, i % 4, :, :], Bb[:, hn * NH:hn * NH + NH, :],
                                    du[:, j % 2, :].unsqueeze(1).to_broadcast([P, NH, TB]),
                                    ALU.mult).then_inc(s_mul, 1)
                    dve.wait_ge(s_e0, NJ * c + j + 1)
                    after(dve, s_hprev, NK * c + i)
                    V.tensor_tensor(c0[:, i % 2, :], e0[:, j % 2, hn * NH:hn * NH + NH],
                                    hprev[:, j, hn * NH:hn * NH + NH], ALU.mult).then_inc(s_c0, 1)
                elif s == "add0":
                    dve.wait_ge(s_c0, NK * c + i + 1)
                    dve.wait_ge(s_mul, NK * c + i + 1)
                    V.tensor_tensor(bs[:, i % 4, :, 0:1], bs[:, i % 4, :, 0:1], c0[:, i % 2, :].unsqueeze(2),
                                    ALU.add).then_inc(s_add0, 1)
                elif s == "scan":
                    dve.wait_ge(s_exp, NK * c + i + 1)
                    dve.wait_ge(s_add0, NK * c + i + 1)
                    flat = bs[:, i % 4, :, :].rearrange("p n t -> p (n t)")
                    V.tensor_tensor_scan(flat, dA[:, i % 2, :, :].rearrange("p n t -> p (n t)"), flat, 0.0, ALU.mult,
                                         ALU.add).then_inc(s_scan, 1)
                elif s == "save":
                    dve.wait_ge(s_scan, NK * c + i + 1)
                    V.tensor_copy(hprev[:, i // 2, (i % 2) * NH:(i % 2) * NH + NH].unsqueeze(2),
                                  bs[:, i % 4, :, TB - 1:TB]).then_inc(s_hprev, 1)
                elif s == "fold":
                    dve.wait_ge(s_cmul, NK * c + i + 1)
                    for n, half in enumerate((NH // 2, NH // 4)):
                        if n:
                            dve.wait_ge(s_fold, 2 * NK * c + 2 * i + 1)
                        V.tensor_tensor(bs[:, i % 4, 0:half, :], bs[:, i % 4, 0:half, :],
                                        bs[:, i % 4, half:2 * half, :], ALU.add).then_inc(s_fold, 1)
                elif s == "fin":
                    dve.wait_ge(s_red, NK * c + 2 * i + 2)
                    dve.wait_ge(s_skip, NJ * c + i + 1)
                    V.tensor_tensor(z[:, i, :], z[:, i, :], ybank[:, 0, :], ALU.add).then_inc(s_fa, 1)
                    dve.wait_ge(s_fa, NJ * c + i + 1)
                    dve.wait_ge(s_gg, NJ * c + i + 1)
                    V.tensor_tensor(z[:, i, :], z[:, i, :], gg[:, i % 4, :], ALU.mult).then_inc(s_z, 1)
                elif s == "out":
                    dve.wait_ge(s_wo, 4 * c + 4)
                    dve.wait_ge(s_keepx, KH * c + KH)
                    after(dve, s_store, 16 * c)
                    for mt in range(KH):
                        V.tensor_tensor(sq[:, mt, :], acc[mt // 2][:, mt % 2, :], xres[:, mt, :],
                                        ALU.add).then_inc(s_out, 1)

            run(dve, VECTOR, stepper(step))

        @block.scalar
        def _(act):
            A = nc.scalar.activation
            act.preload_act_table_set("natural_log_exp_and_others")
            act.wait_ge(s_res, 16 * NRESDMA)
            A(cm[:, :], disc, ACT.Exp, scale=-1.0).then_inc(s_setup_act, 1)
            act.wait_ge(s_setup_dve, 4)
            A(negA[:, :, :], negA[:, :, :], ACT.Exp).then_inc(s_setup_act, 1)

            def sigmoid(out, src, sem_, at):
                A(out, src, ACT.Exp, scale=-1.0).then_inc(sem_, 1)
                act.wait_ge(sem_, at + 1)
                A(out, out, ACT.Ln, bias=1.0).then_inc(sem_, 1)
                act.wait_ge(sem_, at + 2)
                A(out, out, ACT.Exp, scale=-1.0).then_inc(sem_, 1)

            def step(s, i, c, _n):
                if s == "xload":
                    act.wait_ge(s_x1, KH * c)
                    act.dma_start(x_in[:, :, :], xT[:, :, bass.ds(c * TB, TB)]).then_inc(s_x, 16)
                elif s == "store":
                    act.wait_ge(s_out, KH * c + KH)
                    act.dma_start(outT[:, :, bass.ds(c * TB, TB)], sq[:, :, :]).then_inc(s_store, 16)
                elif s in ("mean0", "mean1"):
                    l = int(s[-1])
                    act.wait_ge(s_xc[l], c + 1)
                    if l == 0:
                        after(act, s_store, 16 * c - 16)
                    A(sq[:, :, :], (xn0, xn1)[l][:, :, :], ACT.Square).then_inc(s_sq[l], 1)
                elif s in ("var0", "var1"):
                    l = int(s[-1])
                    act.wait_ge(s_var[l], c + 1)
                    A(rstd[:, :], small[:, 1, :], ACT.Ln, bias=cst[:, K_EPS:K_EPS + 1]).then_inc(s_rstd[l], 1)
                    act.wait_ge(s_rstd[l], 2 * c + 1)
                    A(rstd[:, :], rstd[:, :], ACT.Exp, scale=-0.5).then_inc(s_rstd[l], 1)
                elif s == "updelta":
                    act.wait_ge(s_ud, c + 1)
                    after(act, s_acc0, c)
                    act.wait_ge(s_setup_dve, 5)
                    A(up[:, :], pair[0][:, 0, :], ACT.Copy).then_inc(s_uds, 1)
                    A(delta[:, :], pair[0][:, 1, :], ACT.Identity, bias=nlp[:, :]).then_inc(s_uds, 1)
                    A(keep[:, :], pair[0][:, 1, :], ACT.Abs, bias=nlp[:, :]).then_inc(s_uds, 1)
                elif s == "power":
                    act.wait_ge(s_pow, 9 * c + 7)
                    for g in range(MIN_ORDER):
                        A(q[:, g, :], q[:, g, :], ACT.Copy, scale=cm[:, g:g + 1]).then_inc(s_tay, 1)
                elif s == "experts":
                    act.wait_ge(s_lora, c + 1)
                    A(hw[:, :], pair[1][:, 0, :], ACT.Copy).then_inc(s_wt, 1)
                elif s == "gu":
                    act.wait_ge(s_gcl, NF * c + i + 1)
                    sigmoid(sig[:, i % 3, :], gcl[:, i % 3, :], s_sig, 3 * (NF * c + i))
                elif s == "winx":
                    act.wait_ge(s_winx, 4 * c + i + 1)
                    after(act, s_conv, 40 * c + 10 * i - 10)
                    A(xpad[:, 2 * (i % 2):2 * (i % 2) + 2, KC - 1:], pair[i % 2][:, :, :], ACT.Copy).then_inc(s_xpad, 1)
                elif s == "csilu":
                    for d in range(2):
                        j = 2 * i + d
                        act.wait_ge(s_conv, 40 * c + 10 * i + 9 + d)
                        if j >= 2:
                            act.wait_ge(s_u, NJ * c + j - 1)
                        sigmoid(cs[:, d, :], cv[:, j % 4, :], s_csig, 3 * (NJ * c + j))
                elif s == "wx":
                    act.wait_ge(s_ssm, c + 1)
                    A(ssm, small[:, 0, :], ACT.Copy).then_inc(s_ssq, 1)
                    A(sq[:, 0, :], small[:, 0, :], ACT.Square).then_inc(s_ssq, 1)
                elif s == "rms":
                    act.wait_ge(s_rms, c + 1)
                    A(rr, small[:, 1, :], ACT.Ln, bias=cst[:, K_EPS + 1:K_EPS + 2]).then_inc(s_rr, 1)
                    act.wait_ge(s_rr, 2 * c + 1)
                    A(rr, rr, ACT.Exp, scale=-0.5).then_inc(s_rr, 1)
                elif s == "bc":
                    for r in range(4 * i, 4 * i + 4):
                        n, which = bc_rows(r)
                        act.wait_ge(s_bc, NK * c + r + 1)
                        after(act, s_cmul if which else s_mul, NK * c - 1 + i // 2)
                        A((Cb if which else Bb)[:, n:n + 2, :], pair[r % 2][:, :, :], ACT.Copy).then_inc(s_bce, 1)
                elif s == "dg_a":
                    act.wait_ge(s_dg, NJ * c + i + 1)
                    after(act, s_dt, NJ * c + i)
                    A(xb[:, :], side[:, 0, :], ACT.Identity, bias=vec(V_BDT + i)).then_inc(s_xb, 1)
                    act.wait_ge(s_xb, NJ * c + i + 1)
                    A(ee[:, :], xb[:, :], ACT.Abs).then_inc(s_e, 1)
                    act.wait_ge(s_e, 2 * NJ * c + 2 * i + 1)
                    A(ee[:, :], ee[:, :], ACT.Exp, scale=-1.0).then_inc(s_e, 1)
                elif s == "dg_b":
                    act.wait_ge(s_gcg, NJ * c + i + 1)
                    after(act, s_gg, NJ * c + i)
                    sigmoid(gs[:, :], gg[:, i % 4, :], s_gsig, 3 * (NJ * c + i))
                elif s == "dg_c":
                    act.wait_ge(s_w, 2 * NJ * c + 2 * i + 2)
                    A(ww[:, :], ww[:, :], ACT.Ln).then_inc(s_ln, 1)
                elif s == "skip":
                    after(act, s_wo, 4 * c)
                    A(z[:, i, :], u[:, i, :], ACT.Copy, scale=vec(V_D + i)).then_inc(s_skip, 1)
                elif s == "exp":
                    j, hn = i // 2, i % 2
                    act.wait_ge(s_dt, NJ * c + j + 1)
                    act.wait_ge(s_setup_dve, 6)
                    if hn == 0:
                        after(act, s_c0, NK * c + 2 * j - 2)
                        A(e0[:, j % 2, :], negA[:, j, :], ACT.Exp, scale=dt[:, j % 2, 0:1]).then_inc(s_e0, 1)
                    after(act, s_scan, NK * c + i - 1)
                    for n in range(NH):
                        m = A(dA[:, i % 2, n, 1:TB], dt[:, j % 2, 1:TB], ACT.Exp,
                              scale=negA[:, j, hn * NH + n:hn * NH + n + 1])
                    m.then_inc(s_exp, 1)
                elif s == "ffn1a":
                    act.wait_ge(s_ffn1a, c + 1)
                    A(ha, small[0:RX, 0, :], ACT.Copy, scale=LORA_SCALE).then_inc(s_ha, 1)

            run(act, SCALAR, stepper(step))

        @block.gpsimd
        def _(pool):
            TT = nc.gpsimd.tensor_tensor

            def step(s, i, c, _n):
                if s == "gu":
                    pool.wait_ge(s_sig, 3 * (NF * c + i) + 3)
                    TT(gcl[:, i % 3, :], gcl[:, i % 3, :], sig[:, i % 3, :], ALU.mult).then_inc(s_silu, 1)
                elif s == "csilu":
                    after(pool, s_skip, NJ * c)
                    after(pool, s_du, NJ * c)
                    for d in range(2):
                        j = 2 * i + d
                        pool.wait_ge(s_csig, 3 * (NJ * c + j) + 3)
                        TT(u[:, j, :], cv[:, j % 4, :], cs[:, d, :], ALU.mult).then_inc(s_u, 1)
                elif s == "dg_b":
                    pool.wait_ge(s_gsig, 3 * (NJ * c + i) + 3)
                    TT(gg[:, i % 4, :], gg[:, i % 4, :], gs[:, :], ALU.mult).then_inc(s_gg, 1)
                elif s == "dg_c":
                    pool.wait_ge(s_m, NJ * c + i + 1)
                    after(pool, s_exp, NK * c + 2 * i - 2)
                    TT(dt[:, i % 2, :], xb[:, :], ee[:, :], ALU.subtract).then_inc(s_dt, 1)
                    pool.wait_ge(s_dt, NJ * c + i + 1)
                    after(pool, s_mul, NK * c + 2 * i - 2)
                    TT(du[:, i % 2, :], dt[:, i % 2, :], u[:, i, :], ALU.mult).then_inc(s_du, 1)
                elif s == "cmul":
                    j, hn = i // 2, i % 2
                    pool.wait_ge(s_hprev, NK * c + i + 1)
                    pool.wait_ge(s_bce, NK * c + 8 * hn + 8)
                    TT(bs[:, i % 4, :, :], bs[:, i % 4, :, :], Cb[:, hn * NH:hn * NH + NH, :],
                       ALU.mult).then_inc(s_cmul, 1)

            run(pool, GPSIMD, stepper(step))


_L0A, _L0F, _L1A, _L1F = "L0_attn_", "L0_ffn_", "L1_attn_", "L1_ffn_"


def kernel(**inputs):
    import numpy as np
    import concourse.bacc as _bacc
    from concourse.bass_utils import run_bass_kernel_spmd as _run

    a = {k: np.asarray(v) for k, v in inputs.items()}
    f32 = np.float32

    def rows(w, k):
        return w.reshape(k, P, -1).transpose(1, 0, 2).reshape(P, -1)

    def wide(w, f):
        out = np.zeros((w.shape[0], f), f32)
        out[:, :w.shape[1]] = w
        return out

    def col(v):
        return v.reshape(-1, P).T

    g, up = wide(a[_L0A + "ffn_gate_w"].T, F), wide(a[_L0A + "ffn_up_w"].T, F)
    down = wide(a[_L0A + "ffn_down_w"], F).T
    base, w1, wo = a[_L0F + "W_base"].T, a[_L1F + "w"].T, a[_L1A + "W_out"].T
    w_in = a[_L1A + "W_in"].T
    chunks = np.zeros((NCHUNK, P, CW), f32)
    chunks[UPG] = rows(np.concatenate([a[_L0A + "up_w"].T, a[_L0A + "gate_w"].T], 1), KH)
    for i in range(2):
        chunks[BASE + i] = rows(base[2 * P * i:2 * P * (i + 1)], 2)
        chunks[F1 + i] = rows(w1[2 * P * i:2 * P * (i + 1)], 2)
    for i in range(NF):
        chunks[GU + i] = rows(np.concatenate([g[:, P * i:P * (i + 1)], up[:, P * i:P * (i + 1)]], 1), KH)
    w_x = a[_L1A + "W_x"].T
    chunks[WXP] = rows(np.concatenate([w_x, w_x], 1), NJ)
    for i in range(4):
        chunks[WO + i] = rows(wo[2 * P * i:2 * P * (i + 1)], 2)
        chunks[WX + i] = rows(w_in[:, 2 * P * i:2 * P * (i + 1)], KH)
    down_w = down.reshape(NF, P, H)
    gate_w = np.zeros((NJ, P, H + P), f32)
    for j in range(NJ):
        gate_w[j, :, :H] = rows(w_in[:, DI + P * j:DI + P * (j + 1)], KH)
        gate_w[j, :RT, H:] = a[_L1A + "W_dt"][P * j:P * (j + 1)].T

    res = np.zeros((P, NRES), f32)
    res[:, C_LORA_A:C_LORA_A + KH * P] = rows(a[_L0F + "lora_A"].transpose(1, 0, 2).reshape(H, P), KH)
    res[:, C_LORA_B:C_LORA_B + H] = a[_L0F + "lora_B"].reshape(P, H)
    res[:, C_LAO:C_LAO + H] = a[_L0A + "local_approx_output"].T
    res[:, C_FUSE:C_FUSE + G * H] = a[_L0A + "fuse_weight"].transpose(1, 2, 0).reshape(P, G * H)
    res[:, C_ROUTER:C_ROUTER + KH * E] = rows(a[_L0F + "W_router"].T, KH)
    res[:, C_ALOG:C_ALOG + NJ * NS] = rows(a[_L1A + "A_log"], NJ)
    res[:, C_LA1:C_LA1 + KH * RX] = rows(a[_L1F + "lora_a"], KH)
    v = res[:, C_VEC:]
    v[:, V_LP] = a[_L0A + "local_point"]
    v[:, V_B0:V_B0 + KH] = col(a[_L0F + "b_base"])
    v[:, V_CW:V_CW + NJ * KC] = rows(a[_L1A + "conv_w"], NJ)
    v[:, V_CB:V_CB + NJ] = col(a[_L1A + "conv_b"])
    v[:, V_BDT:V_BDT + NJ] = col(a[_L1A + "b_dt"])
    v[:, V_D:V_D + NJ] = col(a[_L1A + "D"])
    v[:, V_B1:V_B1 + KH] = col(a[_L1F + "b"])
    v[:, V_DISC:V_DISC + G] = a[_L0A + "discount_factor"]
    v[:, V_BR:V_BR + E] = a[_L0F + "b_router"]

    cst = np.zeros((P, NCONST), f32)
    cst[:, K_ID:K_ID + P] = np.eye(P)
    cst[:, K_MEAN:K_MEAN + P] = 1.0 / H
    for lo, n in ((0, RT), (RT, NS), (RT + NS, NS)):
        for twin in (0, P // 2):
            cst[lo:lo + n, K_RMS + twin + lo:K_RMS + twin + lo + n] = 1.0 / n
    for twin in (0, P // 2):
        cst[twin + RT:twin + P // 2, K_PICK:K_PICK + 2 * NS] = np.eye(2 * NS)
    cst[:, K_INV:K_INV + E] = 1.0 / np.arange(1, E + 1)
    cst[:, K_EPS], cst[:, K_EPS + 1] = 1e-5, 1e-6

    arrays = {
        "x_t": rows(a[_L0A + "hidden_states"][0].T, KH).reshape(P, KH, T), "chunks": chunks, "down_w": down_w,
        "gate_w": gate_w, "res": res, "lb1": a[_L1F + "lora_b"], "consts": cst,
    }
    arrays = {k: np.ascontiguousarray(w) for k, w in arrays.items()}
    nc = _bacc.Bacc("TRN2", target_bir_lowering=False, num_devices=1)
    args = [nc.dram_tensor(k, w.shape, F32, kind="ExternalInput").ap() for k, w in arrays.items()]
    out = nc.dram_tensor("out_t", (P, KH, T), F32, kind="ExternalOutput").ap()
    build(nc, *args, out)
    r = _run(nc, [arrays], core_ids=[0])
    got = r.results[0]["out_t"]
    return got.transpose(2, 1, 0).reshape(1, T, H)
```

```python
from contextlib import ExitStack

import concourse.bass as bass
from concourse import mybir

F32 = mybir.dt.float32
F32R = mybir.dt.float32r
ALU = mybir.AluOpType
ACT = mybir.ActivationFunctionType
AX_X = mybir.AxisListType.X

P = 128
T = 1024
TB = 256
NB = T // TB
TC = TB // P
H = 512
KH = H // P
F = 1280
NF = F // P
G = 6
MIN_ORDER = 4
THD = 2.5
E, R0 = 8, 16
DI = 1024
NJ = DI // P
NS = 16
NH = NS // 2
NK = 2 * NJ
KC = 4
RT = 32
RX = 16
LORA_SCALE = 2.0
A_LOG_MAX = 80.0
SP_OPS = 10
FLOOR = -40.0

CW = 1024
UPG, BASE, GU, WXP, F1, WO, WX = 0, 1, 3, 13, 14, 16, 20
NCHUNK = 24
RING = 4

C_LORA_A, C_LORA_B, C_LAO, C_FUSE = 0, 512, 1024, 1536
C_ROUTER = C_FUSE + G * H
C_ALOG = C_ROUTER + KH * E
C_LA1 = C_ALOG + NJ * NS
C_VEC = C_LA1 + KH * RX
V_LP, V_B0, V_CW, V_CB, V_BDT, V_D, V_B1 = 0, 1, 5, 37, 45, 53, 61
V_DISC, V_BR = 65, 71
NRES = C_VEC + V_BR + E

K_ID, K_MEAN, K_RMS, K_INV, K_EPS, K_PICK = 0, 128, 256, 384, 392, 394
NCONST = K_PICK + 2 * NS


TENSOR_START = """
    mean0+ var0+ router+ updelta+ lora+ gu:0+ experts+ base+ gu:1+ gu:2+ gu:3+ down:0+ down:1+ gu:4+ gu:5+
    down:2+ gu:6+ gu:7+ down:3+ gu:8+ down:4+ down:5+ gu:9+ down:6+ down:7+ down:8+ down:9+ taylor+ loraout+
    mean1+ var1+ winx:0+ winx:1+ ffn1a+ winx:2+ winx:3+ ffn1+ wx+ rms+ dg_a:0+ bc:0+ bc:1+ bc:2+ bc:3+
"""
TENSOR_BODY = """
    wout:0- wout:1- wout:2- wout:3- dg_a:1 dg_a:2 mean0+ var0+ dg_a:3 router+ updelta+ lora+ gu:0+ experts+
    base+ gu:1+ gu:2+ gu:3+ down:0+ down:1+ dg_a:4 gu:4+ gu:5+ gu:6+ dg_a:5 down:2+ down:3+ gu:7+ gu:8+
    down:4+ down:5+ gu:9+ down:6+ down:7+ dg_a:6 down:8+ down:9+ taylor+ loraout+ dg_a:7 mean1+ var1+ winx:0+
    ffn1a+ winx:1+ winx:2+ winx:3+ ffn1+ wx+ rms+ dg_a:0+ bc:0+ bc:1+ bc:2+ bc:3+
"""
TENSOR_LAST = """
    wout:0- dg_a:1 wout:1- dg_a:2 wout:2- wout:3- dg_a:3 red:0 red:1 dg_a:4 red:2 red:3 dg_a:5 red:4 red:5
    dg_a:6 wout:0 red:6 red:7 dg_a:7 red:8 red:9 wout:1 red:10 red:11 wout:2 red:12 red:13 red:14 red:15
    wout:3
"""
VECTOR_START = """
    xsum0+ mean0+ sqsum0+ var0+ router+ gu:0+ power+ hmul:0+ experts+ gu:1+ gu:2+ gu:3+ hmul:1+ hmul:2+ gu:4+
    gu:5+ hmul:3+ hmul:4+ hmul:5+ gu:6+ gu:7+ hmul:6+ gu:8+ hmul:7+ hmul:8+ gu:9+ hmul:9+ x1+ xsum1+ mean1+
    sqsum1+ var1+ conv:0+ conv:1+ conv:2+ conv:3+ keepx+ rms+ dg_a:0+ dg_b:0+ dg_c:0+ mul:0+
"""
VECTOR_BODY = """
    scan:0 save:0 mul:1 out- scan:1 dg_a:1 dg_b:1 dg_c:1 xsum0+ dg_a:2 mean0+ dg_b:2 sqsum0+ fold:0 var0+
    save:1 mul:2 scan:2 router+ power+ save:2 gu:0+ fold:1 dg_c:2 mul:3 experts+ scan:3 dg_a:3 hmul:0+ fin:0
    save:3 mul:4 dg_b:3 scan:4 gu:1+ gu:2+ save:4 mul:5 dg_c:3 gu:3+ hmul:1+ fold:2 fold:3 scan:5 hmul:2+
    save:5 fin:1 hmul:3+ mul:6 scan:6 save:6 dg_a:4 dg_b:4 gu:4+ gu:5+ mul:7 hmul:4+ scan:7 fold:4 gu:6+
    dg_c:4 hmul:5+ fold:5 save:7 fin:2 gu:7+ mul:8 hmul:6+ scan:8 gu:8+ save:8 dg_b:5 dg_a:5 hmul:7+ mul:9
    gu:9+ hmul:8+ fold:6 hmul:9+ dg_c:5 fold:7 scan:9 save:9 dg_b:6 fin:3 mul:10 fold:8 scan:10 dg_a:6 fold:9
    save:10 dg_c:6 mul:11 x1+ xsum1+ dg_a:7 mean1+ fin:4 dg_b:7 sqsum1+ scan:11 dg_c:7 var1+ save:11 mul:12
    fold:10 scan:12 fold:11 save:12 conv:0+ conv:1+ mul:13 conv:2+ conv:3+ scan:13 fin:5 save:13 mul:14
    scan:14 rms+ save:14 mul:15 scan:15 save:15 keepx+ fold:12 fold:13 fold:14 fin:6 dg_a:0+ dg_b:0+ dg_c:0+
    fold:15 mul:0+ fin:7
"""
VECTOR_LAST = """
    dg_a:1 dg_b:1 scan:0 dg_c:1 save:0 mul:1 dg_a:2 scan:1 dg_b:2 save:1 mul:2 out- scan:2 dg_c:2 save:2 mul:3
    dg_a:3 scan:3 dg_b:3 fin:0 save:3 mul:4 dg_c:3 scan:4 save:4 mul:5 dg_b:4 scan:5 dg_a:4 save:5 mul:6 fin:1
    scan:6 dg_c:4 save:6 mul:7 dg_a:5 scan:7 dg_b:5 save:7 mul:8 fin:2 scan:8 dg_c:5 save:8 mul:9 dg_a:6
    scan:9 dg_b:6 save:9 mul:10 fin:3 scan:10 dg_c:6 save:10 mul:11 scan:11 dg_b:7 save:11 mul:12 fin:4
    scan:12 dg_c:7 save:12 mul:13 scan:13 fin:5 save:13 mul:14 scan:14 save:14 mul:15 scan:15 save:15 fin:6
    dg_a:7 fin:7 out
"""
SCALAR_START = """
    mean0+ var0+ updelta+ gu:0+ power+ experts+ gu:1+ gu:2+ gu:3+ gu:4+ gu:5+ gu:6+ gu:7+ gu:8+ gu:9+ mean1+
    var1+ winx:0+ winx:1+ csilu:0+ csilu:1+ winx:2+ winx:3+ ffn1a+ csilu:2+ csilu:3+ wx+ rms+ dg_a:0+ bc:0+
    bc:1+ dg_c:0+ bc:2+ exp:0+ bc:3+ dg_b:0+
"""
SCALAR_BODY = """
    exp:1 xload+ store- skip:0 dg_a:1 dg_c:1 dg_a:2 mean0+ dg_c:2 var0+ exp:2 exp:3 updelta+ power+ gu:0+
    experts+ dg_b:1 exp:4 dg_a:3 dg_b:2 exp:5 dg_c:3 gu:1+ gu:2+ skip:1 skip:2 gu:3+ exp:6 dg_a:4 exp:7 dg_c:4
    gu:4+ gu:5+ gu:6+ skip:3 move skip:4 exp:8 dg_a:5 gu:7+ gu:8+ dg_b:3 dg_c:5 skip:5 gu:9+ exp:9 dg_a:6
    dg_b:4 dg_c:6 exp:10 exp:11 dg_a:7 mean1+ dg_b:5 skip:6 dg_c:7 var1+ exp:12 exp:13 dg_b:6 winx:0+ exp:14
    skip:7 winx:1+ csilu:0+ dg_b:7 winx:2+ csilu:1+ winx:3+ csilu:2+ ffn1a+ csilu:3+ wx+ rms+ exp:15 bc:0+
    bc:1+ bc:2+ bc:3+ dg_a:0+ dg_c:0+ dg_b:0+ exp:0+
"""
SCALAR_LAST = """
    dg_a:1 dg_b:1 dg_c:1 exp:1 dg_a:2 exp:2 dg_c:2 exp:3 store- move skip:0 dg_a:3 dg_b:2 exp:4 dg_c:3 skip:1
    exp:5 dg_a:4 dg_b:3 dg_c:4 skip:2 exp:6 exp:7 dg_b:4 dg_a:5 exp:8 skip:3 exp:9 dg_c:5 dg_b:5 dg_a:6 dg_b:6
    exp:10 dg_c:6 exp:11 dg_a:7 skip:4 skip:5 exp:12 dg_c:7 exp:13 exp:14 exp:15 skip:6 skip:7 dg_b:7 store
"""
GPSIMD_START = """
    gu:0+ gu:1+ gu:2+ gu:3+ gu:4+ gu:5+ gu:6+ gu:7+ gu:8+ gu:9+ csilu:0+ csilu:1+ csilu:2+ csilu:3+ dg_c:0+
    dg_b:0+
"""
GPSIMD_BODY = """
    cmul:0 dg_c:1 cmul:1 dg_c:2 dg_b:1 gu:0+ cmul:2 cmul:3 gu:1+ gu:2+ dg_c:3 fin:0 gu:3+ dg_b:2 cmul:4 cmul:5
    gu:4+ gu:5+ cmul:6 fin:1 gu:6+ dg_c:4 cmul:7 gu:7+ gu:8+ gu:9+ dg_b:3 dg_c:5 cmul:8 cmul:9 fin:2 dg_b:4
    fin:3 dg_c:6 cmul:10 dg_b:5 cmul:11 dg_c:7 dg_b:6 cmul:12 csilu:0+ csilu:1+ fin:4 csilu:2+ csilu:3+ fin:5
    dg_b:7 cmul:13 cmul:14 cmul:15 dg_c:0+ fin:6 dg_b:0+ fin:7
"""
GPSIMD_LAST = """
    dg_b:1 dg_c:1 cmul:0 cmul:1 dg_c:2 cmul:2 cmul:3 dg_c:3 dg_b:2 cmul:4 dg_b:3 cmul:5 dg_c:4 cmul:6 dg_b:4
    cmul:7 dg_c:5 dg_b:5 cmul:8 cmul:9 dg_c:6 cmul:10 cmul:11 dg_c:7 cmul:12 cmul:13 cmul:14 cmul:15 dg_b:6
    dg_b:7
"""


def steps(text):
    out = []
    for word in text.split():
        name, _, i = word.rstrip("+-").partition(":")
        out.append(({"+": 1, "-": -1}.get(word[-1], 0), name, int(i or 0)))
    return out


def streamed(order):
    out = []
    for d, s, i in order:
        if s in ("updelta", "wx"):
            out.append(({"updelta": UPG, "wx": WXP}[s], 0, d))
        elif s in ("base", "ffn1"):
            out += [({"base": BASE, "ffn1": F1}[s], kk, d) for kk in range(2)]
        elif s in ("gu", "wout", "winx"):
            out.append(({"gu": GU, "wout": WO, "winx": WX}[s], i, d))
        elif s in ("down", "dg_a"):
            out.append((s, i, d))
    return out


def in_ring(order):
    return [c for c in streamed(order) if c[0] not in ("down", "dg_a")]


class Orders:
    def __init__(self, start, body, last):
        self.start = steps(start)
        self.body = steps(body)
        self.first = [s for s in self.body if s[0] >= 0]
        self.last = steps(last)


def run(eng, orders, stretch):
    stretch(orders.start, 0, -1, 0)
    stretch(orders.first, N0, 0, 0)
    with eng.Fori(1, NB - 1) as b:
        stretch(orders.body, N0 + N1, b, b - 1)
    stretch(orders.last, N0 + N1 + N2 * (NB - 2), NB - 1, 0)


def stepper(step):
    def stretch(order, first, b, turns):
        for d, s, i in order:
            step(s, i, b + d, (first, turns))
            first += len(in_ring([(d, s, i)]))
    return stretch


TENSOR, VECTOR = Orders(TENSOR_START, TENSOR_BODY, TENSOR_LAST), Orders(VECTOR_START, VECTOR_BODY, VECTOR_LAST)
SCALAR, GPSIMD = Orders(SCALAR_START, SCALAR_BODY, SCALAR_LAST), Orders(GPSIMD_START, GPSIMD_BODY, GPSIMD_LAST)
N0, N1, N2 = len(in_ring(TENSOR.start)), len(in_ring(TENSOR.first)), len(in_ring(TENSOR.body))
assert N2 % RING == 0


def bc_rows(i):
    part, r = i // 4, 2 * (i % 4)
    return (part // 2) * NH + r, part % 2


def after(eng, sem, n):
    if not isinstance(n, int) or n > 0:
        eng.wait_ge(sem, n)


def build(nc, xT, chunks, down_w, gate_w, res, lb1, consts, outT):
    with ExitStack() as ctx:
        def sb(name, shape, dtype=F32):
            return ctx.enter_context(nc.sbuf_tensor(name, shape, dtype))

        def bank(name, shape=(P, 2, TB)):
            return ctx.enter_context(nc.psum_tensor(name, list(shape), F32))

        def sem(name):
            return ctx.enter_context(nc.semaphore(name))

        ring = sb("ring", [P, RING, CW])
        resw = sb("resw", [P, NRES])
        down_sb = sb("down_sb", [P, 2, H])
        gate_sb = sb("gate_sb", [P, 2, H + P])
        lb1_sb = sb("lb1_sb", [RX, H])
        cst = sb("cst", [P, NCONST])
        negA = sb("negA", [P, NJ, NS])
        cm = sb("cm", [P, G])
        nlp = sb("nlp", [P, 1])
        ones8 = sb("ones8", [P, E])
        cum = sb("cum", [P, TC, E])
        x_in = sb("x_in", [P, KH, TB])
        x_sb = sb("x_sb", [P, KH, TB])
        xn0 = sb("xn0", [P, KH, TB])
        sq = sb("sq", [P, KH, TB])
        rstd = sb("rstd", [P, TB])
        up = sb("up", [P, TB])
        delta = sb("delta", [P, TB])
        keep = sb("keep", [P, TB])
        q = sb("q", [P, G, TB])
        z8 = sb("z8", [P, TC, E])
        zs = sb("zs", [P, TC, E])
        tau = sb("tau", [P, TC])
        hw = sb("hw", [P, TB])
        gcl = sb("gcl", [P, 3, TB])
        sig = sb("sig", [P, 3, TB])
        h = sb("h", [P, 3, TB])
        xres = sb("xres", [P, KH, TB])
        xn1 = sb("xn1", [P, KH, TB])
        xpad = sb("xpad", [P, 4, TB + KC - 1])
        halo = sb("halo", [P, NJ, KC - 1])
        u = sb("u", [P, NJ, TB])
        z = sb("z", [P, NJ, TB])
        bct = sb("bct", [P, TB])
        bcr = sb("bcr", [P, TB], F32R)
        pick = sb("pick", [P, 2 * NS], F32R)
        Bb = sb("Bb", [P, NS, TB])
        Cb = sb("Cb", [P, NS, TB])
        xb = sb("xb", [P, TB])
        ee = sb("ee", [P, TB])
        ww = sb("ww", [P, TB])
        gs = sb("gs", [P, TB])
        gg = sb("gg", [P, 4, TB])
        dt = sb("dt", [P, 2, TB])
        du = sb("du", [P, 2, TB])
        hprev = sb("hprev", [P, NJ, NS])
        dA = sb("dA", [P, 2, NH, 1 + TB])
        bs = sb("bs", [P, 4, NH, 1 + TB])

        wrep = sig[:, 2, :].rearrange("p (a b) -> p a b", a=TC)
        cv, cs = q[:, 0:4, :], sig[:, 0:2, :]
        ssm, rr = h[:, 0, :], h[:, 1, :]
        ha = hw[0:RX, :]

        def vec(i, rows=P):
            return resw[0:rows, C_VEC + i:C_VEC + i + 1]

        ident = cst[:, K_ID:K_ID + P]
        mean_w = cst[:, K_MEAN:K_MEAN + P]
        rms_w = cst[:, K_RMS:K_RMS + P]
        inv_k = cst[:, K_INV:K_INV + E]
        lora_a = resw[:, C_LORA_A:C_LORA_A + KH * P].rearrange("p (k m) -> p k m", k=KH)
        lora_b = resw[:, C_LORA_B:C_LORA_B + H]
        lao = resw[:, C_LAO:C_LAO + H]
        fuse = resw[:, C_FUSE:C_FUSE + G * H].rearrange("p (g m) -> p g m", g=G)
        router = resw[:, C_ROUTER:C_ROUTER + KH * E].rearrange("p (k m) -> p k m", k=KH)
        a_log = resw[:, C_ALOG:C_ALOG + NJ * NS]
        la1 = resw[:, C_LA1:C_LA1 + KH * RX].rearrange("p (k m) -> p k m", k=KH)
        disc = resw[:, C_VEC + V_DISC:C_VEC + V_DISC + G]
        b_router = resw[:, C_VEC + V_BR:C_VEC + V_BR + E]

        pair = [bank("pair0"), bank("pair1"), bank("pair2")]
        acc = [bank("acc0"), bank("acc1")]
        ybank = bank("ybank")
        small = bank("small")
        side = bank("side")

        s_cst, s_res, s_bigres = sem("s_cst"), sem("s_res"), sem("s_bigres")
        s_setup_act, s_setup_dve = sem("s_setup_act"), sem("s_setup_dve")
        s_chunk = [sem(f"s_chunk{i}") for i in range(RING)]
        s_downw = [sem("s_downw0"), sem("s_downw1")]
        s_gatew = [sem("s_gatew0"), sem("s_gatew1")]
        s_basew, s_f1w, s_wo = sem("s_basew"), sem("s_f1w"), sem("s_wo")
        s_x = sem("s_x")
        s_mean = [sem("s_mean0"), sem("s_mean1")]
        s_xsum = [sem("s_xsum0"), sem("s_xsum1")]
        s_sqsum = [sem("s_sqsum0"), sem("s_sqsum1")]
        s_xc = [sem("s_xc0"), sem("s_xc1")]
        s_sq = [sem("s_sq0"), sem("s_sq1")]
        s_var = [sem("s_var0"), sem("s_var1")]
        s_rstd = [sem("s_rstd0"), sem("s_rstd1")]
        s_xn = [sem("s_xn0"), sem("s_xn1")]
        s_router, s_sparse = sem("s_router"), sem("s_sparse")
        s_ud, s_uds, s_pow, s_tay = sem("s_ud"), sem("s_uds"), sem("s_pow"), sem("s_tay")
        s_lora, s_wt, s_hw = sem("s_lora"), sem("s_wt"), sem("s_hw")
        s_gu, s_gcl, s_sig, s_silu, s_h, s_down = (sem("s_gu"), sem("s_gcl"), sem("s_sig"), sem("s_silu"),
                                                  sem("s_h"), sem("s_down"))
        s_acc0, s_x1, s_keepx, s_move = sem("s_acc0"), sem("s_x1"), sem("s_keepx"), sem("s_move")
        s_winx, s_xpad, s_tap, s_conv, s_csig, s_u, s_halo = (
            sem("s_winx"), sem("s_xpad"), sem("s_tap"), sem("s_conv"), sem("s_csig"), sem("s_u"), sem("s_halo"))
        s_ssm, s_ssq, s_rms, s_rr, s_bct = sem("s_ssm"), sem("s_ssq"), sem("s_rms"), sem("s_rr"), sem("s_bct")
        s_pick, s_bc, s_bce = sem("s_pick"), sem("s_bc"), sem("s_bce")
        s_dg, s_xb, s_gcg, s_e, s_w, s_ln, s_m = (sem("s_dg"), sem("s_xb"), sem("s_gcg"), sem("s_e"), sem("s_w"),
                                                  sem("s_ln"), sem("s_m"))
        s_dt, s_du, s_gsig, s_gg = sem("s_dt"), sem("s_du"), sem("s_gsig"), sem("s_gg")
        s_exp, s_mul, s_head, s_scan, s_hprev, s_cmul, s_fold, s_skip, s_red, s_fa, s_z = (
            sem("s_exp"), sem("s_mul"), sem("s_head"), sem("s_scan"), sem("s_hprev"),
            sem("s_cmul"), sem("s_fold"), sem("s_skip"), sem("s_red"), sem("s_fa"), sem("s_z"))
        s_ffn1a, s_ha, s_ffn1, s_out, s_store = (sem("s_ffn1a"), sem("s_ha"), sem("s_ffn1"), sem("s_out"),
                                                 sem("s_store"))

        block = ctx.enter_context(nc.Block())

        @block.sync
        def _(sp):
            def ring_used(kind, i, c):
                sem_, n = {UPG: (s_ud, c + 1), BASE: (s_basew, 2 * c + i + 1), GU: (s_gu, NF * c + i + 1),
                           WXP: (s_ssm, c + 1), F1: (s_f1w, 2 * c + i + 1), WO: (s_wo, 4 * c + i + 1),
                           WX: (s_winx, 4 * c + i + 1)}[kind]
                sp.wait_ge(sem_, n)

            def loads(order, first, b, before):
                ahead = list(before)
                for kind, i, d in streamed(order):
                    c = b + d
                    if kind == "down":
                        after(sp, s_down, NF * c + i - 1)
                        sp.dma_start(down_sb[:, i % 2, :], down_w[i]).then_inc(s_downw[i % 2], 16)
                    elif kind == "dg_a":
                        after(sp, s_dg, NJ * c + i - 1)
                        sp.dma_start(gate_sb[:, i % 2, :], gate_w[i]).then_inc(s_gatew[i % 2], 16)
                    else:
                        if len(ahead) >= RING:
                            ring_used(*ahead[-RING])
                        slot = first % RING
                        sp.dma_start(ring[:, slot, :], chunks[kind + i]).then_inc(s_chunk[slot], 16)
                        ahead.append((kind, i, c))
                        first += 1

            def stretch(order, first, b, _turns):
                before = {id(TENSOR.start): [], id(TENSOR.first): TENSOR.start}.get(id(order), TENSOR.body)
                loads(order, first, b, [(kind, i, b - 1 + d) for kind, i, d in in_ring(before)][-RING:])

            sp.dma_start(x_in[:, :, :], xT[:, :, 0:TB]).then_inc(s_x, 16)
            sp.dma_start(cst[:, :], consts).then_inc(s_cst, 16)
            sp.dma_start(resw[:, C_ROUTER:], res[:, C_ROUTER:]).then_inc(s_res, 16)
            run(sp, TENSOR, stretch)
            sp.wait_ge(s_store, 16 * NB)

        @block.tensor
        def _(pe):
            pe.wait_ge(s_cst, 16)

            def chunk(n, more=0):
                at = n[0] + more
                pe.wait_ge(s_chunk[at % RING], 16 * (at // RING + 1) + 16 * (N2 // RING) * n[1])
                return ring[:, at % RING, :]

            def mm(out, w, x, start, stop):
                return nc.tensor.matmul(out, w, x, start=start, stop=stop, skip_group_check=True)

            def step(s, i, c, t):
                if s in ("mean0", "mean1"):
                    l = int(s[-1])
                    pe.wait_ge(s_xsum[l], 2 * c + 2)
                    mm(small[:, 0, :], mean_w, sq[:, 0, :], True, True).then_inc(s_mean[l], 1)
                elif s in ("var0", "var1"):
                    l = int(s[-1])
                    pe.wait_ge(s_sqsum[l], 2 * c + 2)
                    mm(small[:, 1, :], mean_w, sq[:, 0, :], True, True).then_inc(s_var[l], 1)
                elif s == "router":
                    pe.wait_ge(s_xn[0], c + 1)
                    pe.wait_ge(s_res, 16)
                    for tc in range(TC):
                        for k in range(KH):
                            m = mm(small[:, 0, tc * E:(tc + 1) * E], xn0[:, k, tc * P:(tc + 1) * P],
                                   router[:, k, :], k == 0, k == KH - 1)
                    m.then_inc(s_router, 1)
                elif s == "updelta":
                    after(pe, s_bce, NK * c)
                    w = chunk(t).rearrange("p (k m) -> p k m", k=KH)
                    for half in range(2):
                        for k in range(KH):
                            m = mm(pair[0][:, half, :], w[:, k, half * P:(half + 1) * P], xn0[:, k, :],
                                   k == 0, k == KH - 1)
                    m.then_inc(s_ud, 1)
                elif s == "lora":
                    pe.wait_ge(s_bigres, 32)
                    for k in range(KH):
                        m = mm(pair[1][:, 1, :], lora_a[:, k, :], xn0[:, k, :], k == 0, k == KH - 1)
                elif s == "experts":
                    pe.wait_ge(s_sparse, SP_OPS * c + SP_OPS)
                    for tc in range(TC):
                        m = nc.tensor.matmul(pair[1][:, 0, tc * P:(tc + 1) * P], wrep[:, tc, :], ident,
                                             start=True, stop=True, is_transpose=True, skip_group_check=True)
                    m.then_inc(s_lora, 1)
                elif s == "gu":
                    if i == 0:
                        pe.wait_ge(s_uds, 3 * c + 3)
                    elif i == 1:
                        pe.wait_ge(s_hw, c + 1)
                    else:
                        after(pe, s_h, NF * c + i - 2 if i > 2 else NF * c)
                    w = chunk(t).rearrange("p (k m) -> p k m", k=KH)
                    for half in range(2):
                        for k in range(KH):
                            m = mm(pair[i % 3][:, half, :], w[:, k, half * P:(half + 1) * P], xn0[:, k, :],
                                   k == 0, k == KH - 1)
                    m.then_inc(s_gu, 1)
                elif s == "base":
                    after(pe, s_keepx, KH * c)
                    after(pe, s_out, KH * c - KH)
                    for kk in range(2):
                        w = chunk(t, kk).rearrange("p (k m) -> p k m", k=2)
                        for k in range(2):
                            for mt in range(KH):
                                m = mm(acc[mt // 2][:, mt % 2, :], w[:, k, mt * P:(mt + 1) * P],
                                       xn0[:, 2 * kk + k, :], kk == 0 and k == 0 and mt % 2 == 0, False)
                        m.then_inc(s_basew, 1)
                elif s == "down":
                    pe.wait_ge(s_h, NF * c + i + 1)
                    pe.wait_ge(s_downw[i % 2], 16 * (NF // 2) * c + 16 * (i // 2 + 1))
                    for mt in range(KH):
                        m = mm(acc[mt // 2][:, mt % 2, :], down_sb[:, i % 2, mt * P:(mt + 1) * P], h[:, i % 3, :],
                               False, False)
                    m.then_inc(s_down, 1)
                elif s == "taylor":
                    for mt in range(KH):
                        m = mm(acc[mt // 2][:, mt % 2, :], lao[:, mt * P:(mt + 1) * P], up[:, :], False, False)
                    pe.wait_ge(s_tay, 4 * c + 4)
                    pe.wait_ge(s_pow, 9 * c + 9)
                    for g in range(G):
                        for mt in range(KH):
                            m = mm(acc[mt // 2][:, mt % 2, :], fuse[:, g, mt * P:(mt + 1) * P], q[:, g, :],
                                   False, False)
                elif s == "loraout":
                    pe.wait_ge(s_hw, c + 1)
                    for mt in range(KH):
                        m = mm(acc[mt // 2][:, mt % 2, :], lora_b[:, mt * P:(mt + 1) * P], hw[:, :],
                               False, True)
                    m.then_inc(s_acc0, 1)
                elif s == "winx":
                    pe.wait_ge(s_xn[1], c + 1)
                    if i >= 2:
                        pe.wait_ge(s_tap, 8 * c + 2 * i - 2)
                    else:
                        pe.wait_ge(s_h, NF * c + NF)
                    w = chunk(t).rearrange("p (k m) -> p k m", k=KH)
                    for half in range(2):
                        for k in range(KH):
                            m = mm(pair[i % 2][:, half, :], w[:, k, half * P:(half + 1) * P], xn1[:, k, :],
                                   k == 0, k == KH - 1)
                    m.then_inc(s_winx, 1)
                elif s == "wx":
                    w_x = chunk(t).rearrange("p (k m) -> p k m", k=NJ)
                    pe.wait_ge(s_ha, c + 1)
                    for k in range(NJ):
                        pe.wait_ge(s_u, 4 * c + k // 2 + 1)
                        m = mm(small[:, 0, :], w_x[:, k, :], u[:, k, :], k == 0, k == NJ - 1)
                    m.then_inc(s_ssm, 1)
                elif s == "rms":
                    pe.wait_ge(s_ssq, 2 * c + 2)
                    mm(small[:, 1, :], rms_w, sq[:, 0, :], True, True).then_inc(s_rms, 1)
                elif s == "bc":
                    for r in range(4 * i, 4 * i + 4):
                        if r < 2:
                            pe.wait_ge(s_bct, 3 * c + 3)
                            pe.wait_ge(s_tap, 8 * c + 8)
                            pe.wait_ge(s_pick, 1)
                        else:
                            pe.wait_ge(s_bce, NK * c + r - 1)
                        for half in range(2):
                            n, which = bc_rows(r)
                            row = NS * which + n + half
                            m = mm(pair[r % 2][:, half, :],
                                   pick[:, row:row + 1].to_broadcast([P, P]), bcr[:, :], True, True)
                        m.then_inc(s_bc, 1)
                elif s == "dg_a":
                    pe.wait_ge(s_bct, 3 * c + 1)
                    after(pe, s_gcg, NJ * c + i)
                    after(pe, s_xb, NJ * c + i)
                    pe.wait_ge(s_gatew[i % 2], 16 * (NJ // 2) * c + 16 * (i // 2 + 1))
                    mm(side[:, 0, :], gate_sb[0:RT, i % 2, H:H + P], bct[0:RT, :], True, True)
                    for k in range(KH):
                        m = mm(side[:, 1, :], gate_sb[:, i % 2, k * P:(k + 1) * P], xn1[:, k, :],
                               k == 0, k == KH - 1)
                    m.then_inc(s_dg, 1)
                elif s == "red":
                    j, hn = i // 2, i % 2
                    pe.wait_ge(s_cmul, NK * c + i + 1)
                    if hn == 0 and j:
                        pe.wait_ge(s_fa, NK * c + j)
                    for n in range(NH):
                        m = mm(ybank[:, 0, :], ident, bs[:, i % 4, n, 1:], hn == 0 and n == 0,
                               hn == 1 and n == NH - 1)
                    m.then_inc(s_red, 1)
                elif s == "ffn1a":
                    pe.wait_ge(s_xn[1], c + 1)
                    for k in range(KH):
                        m = mm(small[0:RX, 0, :], la1[:, k, :], xn1[:, k, :], k == 0, k == KH - 1)
                    m.then_inc(s_ffn1a, 1)
                elif s == "ffn1":
                    pe.wait_ge(s_x1, KH * c + KH)
                    for kk in range(2):
                        w = chunk(t, kk).rearrange("p (k m) -> p k m", k=2)
                        for k in range(2):
                            for mt in range(KH):
                                m = mm(acc[mt // 2][:, mt % 2, :], w[:, k, mt * P:(mt + 1) * P],
                                       xn1[:, 2 * kk + k, :], kk == 0 and k == 0 and mt % 2 == 0, False)
                        m.then_inc(s_f1w, 1)
                    pe.wait_ge(s_ha, c + 1)
                    for mt in range(KH):
                        m = mm(acc[mt // 2][:, mt % 2, :], lb1_sb[:, mt * P:(mt + 1) * P], ha, False, True)
                    m.then_inc(s_ffn1, 1)
                elif s == "wout":
                    if isinstance(c, int) and c == NB - 1:
                        pe.wait_ge(s_out, KH * c)
                    else:
                        pe.wait_ge(s_keepx, KH * c + 2 * KH)
                    pe.wait_ge(s_z, NJ * c + 2 * i + 2)
                    w = chunk(t).rearrange("p (k m) -> p k m", k=2)
                    for k in range(2):
                        for mt in range(KH):
                            m = mm(acc[mt // 2][:, mt % 2, :], w[:, k, mt * P:(mt + 1) * P], z[:, 2 * i + k, :],
                                   i == 0 and k == 0 and mt % 2 == 0, i == 3 and k == 1)
                    m.then_inc(s_wo, 1)

            run(pe, TENSOR, stepper(step))

        @block.vector
        def _(dve):
            V = nc.vector
            V.memset(hprev[:, :, :], 0.0).then_inc(s_setup_dve, 1)
            V.memset(dA[:, :, :, 0:1], 0.0).then_inc(s_setup_dve, 1)
            V.memset(ones8[:, :], 1.0).then_inc(s_setup_dve, 1)
            V.memset(halo[:, :, :], 0.0).then_inc(s_halo, 1)
            dve.wait_ge(s_res, 16)
            V.tensor_scalar(negA[:, :, :].rearrange("p j n -> p (j n)"), a_log, A_LOG_MAX, None,
                            ALU.min).then_inc(s_setup_dve, 1)
            V.tensor_scalar(nlp[:, :], vec(V_LP), -1.0, None, ALU.mult).then_inc(s_setup_dve, 1)
            V.tensor_copy(pick[:, :], cst[:, K_PICK:K_PICK + 2 * NS]).then_inc(s_pick, 1)
            dve.wait_ge(s_setup_act, 2)
            V.tensor_scalar(negA[:, :, :], negA[:, :, :], -1.0, None, ALU.mult).then_inc(s_setup_dve, 1)

            def add_up(src, sem_, n):
                V.tensor_tensor(sq[:, 0:2, :], src[:, 0:2, :], src[:, 2:4, :], ALU.add).then_inc(sem_, 1)
                dve.wait_ge(sem_, n + 1)
                V.tensor_tensor(sq[:, 0, :], sq[:, 0, :], sq[:, 1, :], ALU.add).then_inc(sem_, 1)

            def step(s, i, c, _n):
                if s == "xsum0":
                    dve.wait_ge(s_x, 16 * c + 16)
                    after(dve, s_store, 16 * c - 16)
                    add_up(x_in, s_xsum[0], 2 * c)
                elif s == "xsum1":
                    dve.wait_ge(s_x1, KH * c + KH)
                    add_up(x_sb, s_xsum[1], 2 * c)
                elif s in ("sqsum0", "sqsum1"):
                    l = int(s[-1])
                    dve.wait_ge(s_sq[l], c + 1)
                    add_up(sq, s_sqsum[l], 2 * c)
                elif s in ("mean0", "mean1"):
                    l = int(s[-1])
                    xn = (xn0, xn1)[l]
                    dve.wait_ge(s_mean[l], c + 1)
                    if l == 1:
                        after(dve, s_dg, NJ * c)
                        after(dve, s_ffn1, c)
                    V.tensor_tensor(xn[:, :, :], (x_in, x_sb)[l][:, :, :],
                                    small[:, 0, :].unsqueeze(1).to_broadcast([P, KH, TB]),
                                    ALU.subtract).then_inc(s_xc[l], 1)
                elif s in ("var0", "var1"):
                    l = int(s[-1])
                    xn = (xn0, xn1)[l]
                    dve.wait_ge(s_rstd[l], 2 * c + 2)
                    V.tensor_tensor(xn[:, :, :], xn[:, :, :], rstd[:, :].unsqueeze(1).to_broadcast([P, KH, TB]),
                                    ALU.mult).then_inc(s_xn[l], 1)
                elif s == "router":
                    dve.wait_ge(s_router, c + 1)
                    at = SP_OPS * c
                    V.tensor_tensor(z8[:, :, :], small[:, 0, 0:TC * E].rearrange("p (a b) -> p a b", a=TC),
                                    b_router.unsqueeze(1).to_broadcast([P, TC, E]), ALU.add).then_inc(s_sparse, 1)
                    dve.wait_ge(s_sparse, at + 1)
                    V.tensor_copy(cum[:, :, :], z8[:, :, :])
                    for tc in range(TC):
                        V.max(zs[:, tc, :], z8[:, tc, :]).then_inc(s_sparse, 1)
                    for tc in range(TC):
                        dve.wait_ge(s_sparse, at + 2 + tc)
                        V.tensor_tensor_scan(cum[:, tc, :], ones8[:, :], zs[:, tc, :], 0.0, ALU.mult,
                                             ALU.add).then_inc(s_sparse, 1)
                    dve.wait_ge(s_sparse, at + 5)
                    V.scalar_tensor_tensor(zs[:, :, :], cum[:, :, :], -1.0,
                                           inv_k.unsqueeze(1).to_broadcast([P, TC, E]), ALU.add,
                                           ALU.mult).then_inc(s_sparse, 1)
                    dve.wait_ge(s_sparse, at + 6)
                    V.tensor_reduce(tau[:, :], zs[:, :, :], AX_X, ALU.max).then_inc(s_sparse, 1)
                    dve.wait_ge(s_sparse, at + 7)
                    for tc in range(TC):
                        V.tensor_scalar(z8[:, tc, :], z8[:, tc, :], tau[:, tc:tc + 1], 0.0, ALU.subtract,
                                        ALU.max).then_inc(s_sparse, 1)
                    dve.wait_ge(s_sparse, at + 9)
                    V.tensor_copy(wrep[:, :, :].rearrange("p a (e r) -> p a e r", e=E),
                                  z8[:, :, :].unsqueeze(3).to_broadcast([P, TC, E, R0])).then_inc(s_sparse, 1)
                elif s == "power":
                    dve.wait_ge(s_uds, 3 * c + 3)
                    V.tensor_scalar(keep[:, :], keep[:, :], THD, None, ALU.is_le).then_inc(s_pow, 1)
                    for g in range(G):
                        if g:
                            dve.wait_ge(s_pow, 9 * c + g + 1)
                        V.tensor_tensor(q[:, g, :], q[:, g - 1, :] if g else up[:, :], delta[:, :],
                                        ALU.mult).then_inc(s_pow, 1)
                    for n, g in enumerate(range(MIN_ORDER, G)):
                        dve.wait_ge(s_pow, 9 * c + 7)
                        V.scalar_tensor_tensor(q[:, g, :], q[:, g, :], cm[:, g:g + 1], keep[:, :], ALU.mult,
                                               ALU.mult).then_inc(s_pow, 1)
                elif s == "experts":
                    dve.wait_ge(s_wt, c + 1)
                    V.tensor_tensor(hw[:, :], pair[1][:, 1, :], hw[:, :], ALU.mult).then_inc(s_hw, 1)
                elif s == "gu":
                    dve.wait_ge(s_gu, NF * c + i + 1)
                    after(dve, s_h, NF * c + i - 2 if i > 2 else NF * c)
                    V.tensor_scalar(gcl[:, i % 3, :], pair[i % 3][:, 0, :], FLOOR, None, ALU.max).then_inc(s_gcl, 1)
                elif s == "hmul":
                    dve.wait_ge(s_silu, NF * c + i + 1)
                    after(dve, s_down, NF * c + i - 2 if i > 2 else NF * c)
                    V.tensor_tensor(h[:, i % 3, :], gcl[:, i % 3, :], pair[i % 3][:, 1, :],
                                    ALU.mult).then_inc(s_h, 1)
                elif s == "x1":
                    dve.wait_ge(s_acc0, c + 1)
                    after(dve, s_move, c)
                    for mt in range(KH):
                        V.scalar_tensor_tensor(x_sb[:, mt, :], acc[mt // 2][:, mt % 2, :], vec(V_B0 + mt),
                                               x_in[:, mt, :], ALU.add, ALU.add).then_inc(s_x1, 1)
                elif s == "conv":
                    dve.wait_ge(s_xpad, 4 * c + i + 1)
                    xp, hl = xpad[:, 2 * (i % 2):2 * (i % 2) + 2, :], halo[:, 2 * i:2 * i + 2, :]
                    dve.wait_ge(s_halo, 8 * c + 2 * i + 1)
                    V.tensor_copy(xp[:, :, 0:KC - 1], hl).then_inc(s_halo, 1)
                    dve.wait_ge(s_halo, 8 * c + 2 * i + 2)
                    V.tensor_copy(hl, xp[:, :, TB:TB + KC - 1]).then_inc(s_halo, 1)
                    for tap in range(KC - 1):
                        for d in range(2):
                            j = 2 * i + d
                            if tap:
                                dve.wait_ge(s_conv, 28 * c + 7 * i + 2 * tap - 1 + d)
                            else:
                                dve.wait_ge(s_tap, 8 * c + 2 * i + 1 + d)
                            V.scalar_tensor_tensor(cv[:, j % 4, :], xp[:, d, tap:tap + TB],
                                                   vec(V_CW + KC * j + tap), cv[:, j % 4, :], ALU.mult,
                                                   ALU.add).then_inc(s_conv, 1)
                    cv2 = cv[:, 2 * (i % 2):2 * (i % 2) + 2, :]
                    dve.wait_ge(s_conv, 28 * c + 7 * i + 6)
                    V.tensor_scalar(cv2, cv2, FLOOR, None, ALU.max).then_inc(s_conv, 1)
                elif s == "rms":
                    dve.wait_ge(s_rr, 2 * c + 2)
                    V.tensor_tensor(bct[:, :], ssm, rr, ALU.mult).then_inc(s_bct, 1)
                    dve.wait_ge(s_bct, 3 * c + 1)
                    V.tensor_copy(bcr[:, :], bct[:, :]).then_inc(s_bct, 1)
                    dve.wait_ge(s_bct, 3 * c + 2)
                    V.tensor_tensor(bcr[P // 2:, :], bct[P // 2:, :], bcr[P // 2:, :].bitcast(F32),
                                    ALU.subtract).then_inc(s_bct, 1)
                elif s == "keepx":
                    dve.wait_ge(s_ffn1, c + 1)
                    for mt in range(KH):
                        V.scalar_tensor_tensor(x_sb[:, mt, :], acc[mt // 2][:, mt % 2, :], vec(V_B1 + mt),
                                               x_sb[:, mt, :], ALU.add, ALU.add).then_inc(s_keepx, 1)
                elif s == "dg_a":
                    dve.wait_ge(s_dg, NJ * c + i + 1)
                    dve.wait_ge(s_xb, NJ * c + i + 1)
                    after(dve, s_z, NJ * c + i - 3)
                    V.tensor_scalar(gg[:, i % 4, :], side[:, 1, :], FLOOR, None, ALU.max).then_inc(s_gcg, 1)
                elif s == "dg_b":
                    dve.wait_ge(s_w, 2 * NJ * c + 2 * i + 1)
                    V.scalar_tensor_tensor(ee[:, :], ww[:, :], -1.0, ee[:, :], ALU.add,
                                           ALU.subtract).then_inc(s_w, 1)
                elif s == "dg_c":
                    dve.wait_ge(s_ln, NJ * c + i + 1)
                    V.scalar_tensor_tensor(xb[:, :], xb[:, :], 0.0, ww[:, :], ALU.max, ALU.add).then_inc(s_m, 1)
                elif s == "mul":
                    j, hn = i // 2, i % 2
                    dve.wait_ge(s_du, NJ * c + j + 1)
                    dve.wait_ge(s_bce, NK * c + 8 * hn + 4)
                    if isinstance(c, int) and c == NB - 1 and i > 3:
                        dve.wait_ge(s_red, i - 3)
                    else:
                        after(dve, s_fa, NK * c + i - 3)
                    V.tensor_tensor(bs[:, i % 4, :, 1:], Bb[:, hn * NH:hn * NH + NH, :],
                                    du[:, j % 2, :].unsqueeze(1).to_broadcast([P, NH, TB]),
                                    ALU.mult).then_inc(s_mul, 1)
                    after(dve, s_hprev, NK * c + i)
                    V.tensor_copy(bs[:, i % 4, :, 0:1],
                                  hprev[:, j, hn * NH:hn * NH + NH].unsqueeze(2)).then_inc(s_head, 1)
                elif s == "scan":
                    dve.wait_ge(s_exp, NK * c + i + 1)
                    dve.wait_ge(s_mul, NK * c + i + 1)
                    dve.wait_ge(s_head, NK * c + i + 1)
                    flat = bs[:, i % 4, :, :].rearrange("p n t -> p (n t)")
                    V.tensor_tensor_scan(flat, dA[:, i % 2, :, :].rearrange("p n t -> p (n t)"), flat, 0.0, ALU.mult,
                                         ALU.add).then_inc(s_scan, 1)
                elif s == "save":
                    dve.wait_ge(s_scan, NK * c + i + 1)
                    V.tensor_copy(hprev[:, i // 2, (i % 2) * NH:(i % 2) * NH + NH].unsqueeze(2),
                                  bs[:, i % 4, :, TB:]).then_inc(s_hprev, 1)
                elif s == "fold":
                    dve.wait_ge(s_cmul, NK * c + i + 1)
                    for n, half in enumerate((NH // 2, NH // 4, NH // 8)):
                        if n:
                            dve.wait_ge(s_fold, 3 * NK * c + 3 * i + n)
                        V.tensor_tensor(bs[:, i % 4, 0:half, 1:], bs[:, i % 4, 0:half, 1:],
                                        bs[:, i % 4, half:2 * half, 1:], ALU.add).then_inc(s_fold, 1)
                elif s == "fin":
                    dve.wait_ge(s_skip, NJ * c + i + 1)
                    if isinstance(c, int) and c == NB - 1:
                        dve.wait_ge(s_red, 2 * i + 2)
                        V.tensor_tensor(z[:, i, :], z[:, i, :], ybank[:, 0, :], ALU.add).then_inc(s_fa, 1)
                        dve.wait_ge(s_fa, NK * c + i + 1)
                        dve.wait_ge(s_gg, NJ * c + i + 1)
                        V.tensor_tensor(z[:, i, :], z[:, i, :], gg[:, i % 4, :], ALU.mult).then_inc(s_z, 1)
                    else:
                        dve.wait_ge(s_fold, 3 * NK * c + 6 * i + 6)
                        for hn in range(2):
                            if hn:
                                dve.wait_ge(s_fa, NK * c + 2 * i + 1)
                            V.tensor_tensor(z[:, i, :], z[:, i, :], bs[:, (2 * i + hn) % 4, 0, 1:],
                                            ALU.add).then_inc(s_fa, 1)
                elif s == "out":
                    dve.wait_ge(s_wo, 4 * c + 4)
                    dve.wait_ge(s_move, c + 1)
                    after(dve, s_store, 16 * c)
                    for mt in range(KH):
                        V.tensor_tensor(sq[:, mt, :], acc[mt // 2][:, mt % 2, :], xres[:, mt, :],
                                        ALU.add).then_inc(s_out, 1)

            run(dve, VECTOR, stepper(step))

        @block.scalar
        def _(act):
            A = nc.scalar.activation
            act.preload_act_table_set("natural_log_exp_and_others")
            act.wait_ge(s_cst, 16)
            act.wait_ge(s_res, 16)
            act.dma_start(resw[:, 0:C_ROUTER], res[:, 0:C_ROUTER]).then_inc(s_bigres, 16)
            act.dma_start(lb1_sb[:, :], lb1).then_inc(s_bigres, 16)
            A(cm[:, :], disc, ACT.Exp, scale=-1.0).then_inc(s_setup_act, 1)
            act.wait_ge(s_setup_dve, 4)
            A(negA[:, :, :], negA[:, :, :], ACT.Exp).then_inc(s_setup_act, 1)

            def sigmoid(out, src, sem_, at):
                A(out, src, ACT.Exp, scale=-1.0).then_inc(sem_, 1)
                act.wait_ge(sem_, at + 1)
                A(out, out, ACT.Ln, bias=1.0).then_inc(sem_, 1)
                act.wait_ge(sem_, at + 2)
                A(out, out, ACT.Exp, scale=-1.0).then_inc(sem_, 1)

            def step(s, i, c, _n):
                if s == "xload":
                    act.wait_ge(s_x1, KH * c)
                    act.dma_start(x_in[:, :, :], xT[:, :, bass.ds(c * TB, TB)]).then_inc(s_x, 16)
                elif s == "store":
                    act.wait_ge(s_out, KH * c + KH)
                    act.dma_start(outT[:, :, bass.ds(c * TB, TB)], sq[:, :, :]).then_inc(s_store, 16)
                elif s in ("mean0", "mean1"):
                    l = int(s[-1])
                    act.wait_ge(s_xc[l], c + 1)
                    A(sq[:, :, :], (xn0, xn1)[l][:, :, :], ACT.Square).then_inc(s_sq[l], 1)
                elif s in ("var0", "var1"):
                    l = int(s[-1])
                    act.wait_ge(s_var[l], c + 1)
                    A(rstd[:, :], small[:, 1, :], ACT.Ln, bias=cst[:, K_EPS:K_EPS + 1]).then_inc(s_rstd[l], 1)
                    act.wait_ge(s_rstd[l], 2 * c + 1)
                    A(rstd[:, :], rstd[:, :], ACT.Exp, scale=-0.5).then_inc(s_rstd[l], 1)
                elif s == "updelta":
                    act.wait_ge(s_ud, c + 1)
                    after(act, s_acc0, c)
                    act.wait_ge(s_setup_dve, 5)
                    A(up[:, :], pair[0][:, 0, :], ACT.Copy).then_inc(s_uds, 1)
                    A(delta[:, :], pair[0][:, 1, :], ACT.Identity, bias=nlp[:, :]).then_inc(s_uds, 1)
                    A(keep[:, :], pair[0][:, 1, :], ACT.Abs, bias=nlp[:, :]).then_inc(s_uds, 1)
                elif s == "power":
                    act.wait_ge(s_pow, 9 * c + 7)
                    for g in range(MIN_ORDER):
                        A(q[:, g, :], q[:, g, :], ACT.Copy, scale=cm[:, g:g + 1]).then_inc(s_tay, 1)
                elif s == "experts":
                    act.wait_ge(s_lora, c + 1)
                    A(hw[:, :], pair[1][:, 0, :], ACT.Copy).then_inc(s_wt, 1)
                elif s == "gu":
                    act.wait_ge(s_gcl, NF * c + i + 1)
                    sigmoid(sig[:, i % 3, :], gcl[:, i % 3, :], s_sig, 3 * (NF * c + i))
                elif s == "winx":
                    act.wait_ge(s_winx, 4 * c + i + 1)
                    after(act, s_conv, 28 * c + 7 * i - 7)
                    A(xpad[:, 2 * (i % 2):2 * (i % 2) + 2, KC - 1:], pair[i % 2][:, :, :], ACT.Copy).then_inc(s_xpad, 1)
                    after(act, s_u, 4 * c + i - 1)
                    for d in range(2):
                        j = 2 * i + d
                        A(cv[:, j % 4, :], pair[i % 2][:, d, :], ACT.Identity, scale=vec(V_CW + KC * j + KC - 1),
                          bias=vec(V_CB + j)).then_inc(s_tap, 1)
                elif s == "csilu":
                    act.wait_ge(s_conv, 28 * c + 7 * i + 7)
                    after(act, s_u, 4 * c + i)
                    sigmoid(cs[:, :, :], cv[:, 2 * (i % 2):2 * (i % 2) + 2, :], s_csig, 3 * (4 * c + i))
                elif s == "wx":
                    act.wait_ge(s_ssm, c + 1)
                    A(ssm, small[:, 0, :], ACT.Copy).then_inc(s_ssq, 1)
                    A(sq[:, 0, :], small[:, 0, :], ACT.Square).then_inc(s_ssq, 1)
                elif s == "rms":
                    act.wait_ge(s_rms, c + 1)
                    A(rr, small[:, 1, :], ACT.Ln, bias=cst[:, K_EPS + 1:K_EPS + 2]).then_inc(s_rr, 1)
                    act.wait_ge(s_rr, 2 * c + 1)
                    A(rr, rr, ACT.Exp, scale=-0.5).then_inc(s_rr, 1)
                elif s == "bc":
                    for r in range(4 * i, 4 * i + 4):
                        n, which = bc_rows(r)
                        act.wait_ge(s_bc, NK * c + r + 1)
                        after(act, s_cmul if which else s_mul, NK * c - 1 + i // 2)
                        A((Cb if which else Bb)[:, n:n + 2, :], pair[r % 2][:, :, :], ACT.Copy).then_inc(s_bce, 1)
                elif s == "dg_a":
                    act.wait_ge(s_dg, NJ * c + i + 1)
                    after(act, s_dt, NJ * c + i)
                    A(xb[:, :], side[:, 0, :], ACT.Identity, bias=vec(V_BDT + i)).then_inc(s_xb, 1)
                    act.wait_ge(s_xb, NJ * c + i + 1)
                    A(ee[:, :], xb[:, :], ACT.Abs).then_inc(s_e, 1)
                    act.wait_ge(s_e, 2 * NJ * c + 2 * i + 1)
                    A(ee[:, :], ee[:, :], ACT.Exp, scale=-1.0).then_inc(s_e, 1)
                    act.wait_ge(s_e, 2 * NJ * c + 2 * i + 2)
                    after(act, s_m, NJ * c + i)
                    A(ww[:, :], ee[:, :], ACT.Identity, bias=1.0).then_inc(s_w, 1)
                elif s == "dg_b":
                    act.wait_ge(s_gcg, NJ * c + i + 1)
                    after(act, s_gg, NJ * c + i)
                    sigmoid(gs[:, :], gg[:, i % 4, :], s_gsig, 3 * (NJ * c + i))
                elif s == "dg_c":
                    act.wait_ge(s_w, 2 * NJ * c + 2 * i + 2)
                    A(ww[:, :], ww[:, :], ACT.Ln).then_inc(s_ln, 1)
                elif s == "skip":
                    after(act, s_wo, 4 * c)
                    A(z[:, i, :], u[:, i, :], ACT.Copy, scale=vec(V_D + i)).then_inc(s_skip, 1)
                elif s == "exp":
                    j, hn = i // 2, i % 2
                    act.wait_ge(s_dt, NJ * c + j + 1)
                    act.wait_ge(s_setup_dve, 6)
                    after(act, s_scan, NK * c + i - 1)
                    for n in range(NH):
                        m = A(dA[:, i % 2, n, 1:], dt[:, j % 2, :], ACT.Exp,
                              scale=negA[:, j, hn * NH + n:hn * NH + n + 1])
                    m.then_inc(s_exp, 1)
                elif s == "move":
                    act.wait_ge(s_keepx, KH * c + KH)
                    after(act, s_out, KH * c)
                    A(xres[:, :, :], x_sb[:, :, :], ACT.Copy).then_inc(s_move, 1)
                elif s == "ffn1a":
                    act.wait_ge(s_ffn1a, c + 1)
                    A(ha, small[0:RX, 0, :], ACT.Copy, scale=LORA_SCALE).then_inc(s_ha, 1)

            run(act, SCALAR, stepper(step))

        @block.gpsimd
        def _(pool):
            TT = nc.gpsimd.tensor_tensor

            def step(s, i, c, _n):
                if s == "gu":
                    pool.wait_ge(s_sig, 3 * (NF * c + i) + 3)
                    TT(gcl[:, i % 3, :], gcl[:, i % 3, :], sig[:, i % 3, :], ALU.mult).then_inc(s_silu, 1)
                elif s == "csilu":
                    after(pool, s_skip, NJ * c)
                    after(pool, s_du, NJ * c)
                    pool.wait_ge(s_csig, 3 * (4 * c + i) + 3)
                    TT(u[:, 2 * i:2 * i + 2, :], cv[:, 2 * (i % 2):2 * (i % 2) + 2, :], cs[:, :, :],
                       ALU.mult).then_inc(s_u, 1)
                elif s == "dg_b":
                    pool.wait_ge(s_gsig, 3 * (NJ * c + i) + 3)
                    TT(gg[:, i % 4, :], gg[:, i % 4, :], gs[:, :], ALU.mult).then_inc(s_gg, 1)
                elif s == "dg_c":
                    pool.wait_ge(s_m, NJ * c + i + 1)
                    after(pool, s_exp, NK * c + 2 * i - 2)
                    TT(dt[:, i % 2, :], xb[:, :], ee[:, :], ALU.subtract).then_inc(s_dt, 1)
                    pool.wait_ge(s_dt, NJ * c + i + 1)
                    after(pool, s_mul, NK * c + 2 * i - 2)
                    TT(du[:, i % 2, :], dt[:, i % 2, :], u[:, i, :], ALU.mult).then_inc(s_du, 1)
                elif s == "fin":
                    pool.wait_ge(s_fa, NK * c + 2 * i + 2)
                    pool.wait_ge(s_gg, NJ * c + i + 1)
                    TT(z[:, i, :], z[:, i, :], gg[:, i % 4, :], ALU.mult).then_inc(s_z, 1)
                elif s == "cmul":
                    j, hn = i // 2, i % 2
                    pool.wait_ge(s_hprev, NK * c + i + 1)
                    pool.wait_ge(s_bce, NK * c + 8 * hn + 8)
                    TT(bs[:, i % 4, :, 1:], bs[:, i % 4, :, 1:], Cb[:, hn * NH:hn * NH + NH, :],
                       ALU.mult).then_inc(s_cmul, 1)

            run(pool, GPSIMD, stepper(step))


_L0A, _L0F, _L1A, _L1F = "L0_attn_", "L0_ffn_", "L1_attn_", "L1_ffn_"


def kernel(**inputs):
    import numpy as np
    import concourse.bacc as _bacc
    from concourse.bass_utils import run_bass_kernel_spmd as _run

    a = {k: np.asarray(v) for k, v in inputs.items()}
    f32 = np.float32

    def rows(w, k):
        return w.reshape(k, P, -1).transpose(1, 0, 2).reshape(P, -1)

    def wide(w, f):
        out = np.zeros((w.shape[0], f), f32)
        out[:, :w.shape[1]] = w
        return out

    def col(v):
        return v.reshape(-1, P).T

    g, up = wide(a[_L0A + "ffn_gate_w"].T, F), wide(a[_L0A + "ffn_up_w"].T, F)
    down = wide(a[_L0A + "ffn_down_w"], F).T
    base, w1, wo = a[_L0F + "W_base"].T, a[_L1F + "w"].T, a[_L1A + "W_out"].T
    w_in = a[_L1A + "W_in"].T
    chunks = np.zeros((NCHUNK, P, CW), f32)
    chunks[UPG] = rows(np.concatenate([a[_L0A + "up_w"].T, a[_L0A + "gate_w"].T], 1), KH)
    for i in range(2):
        chunks[BASE + i] = rows(base[2 * P * i:2 * P * (i + 1)], 2)
        chunks[F1 + i] = rows(w1[2 * P * i:2 * P * (i + 1)], 2)
    for i in range(NF):
        chunks[GU + i] = rows(np.concatenate([g[:, P * i:P * (i + 1)], up[:, P * i:P * (i + 1)]], 1), KH)
    w_x = a[_L1A + "W_x"].T
    chunks[WXP] = rows(np.concatenate([w_x, w_x], 1), NJ)
    for i in range(4):
        chunks[WO + i] = rows(wo[2 * P * i:2 * P * (i + 1)], 2)
        chunks[WX + i] = rows(w_in[:, 2 * P * i:2 * P * (i + 1)], KH)
    down_w = down.reshape(NF, P, H)
    gate_w = np.zeros((NJ, P, H + P), f32)
    for j in range(NJ):
        gate_w[j, :, :H] = rows(w_in[:, DI + P * j:DI + P * (j + 1)], KH)
        gate_w[j, :RT, H:] = a[_L1A + "W_dt"][P * j:P * (j + 1)].T

    res = np.zeros((P, NRES), f32)
    res[:, C_LORA_A:C_LORA_A + KH * P] = rows(a[_L0F + "lora_A"].transpose(1, 0, 2).reshape(H, P), KH)
    res[:, C_LORA_B:C_LORA_B + H] = a[_L0F + "lora_B"].reshape(P, H)
    res[:, C_LAO:C_LAO + H] = a[_L0A + "local_approx_output"].T
    res[:, C_FUSE:C_FUSE + G * H] = a[_L0A + "fuse_weight"].transpose(1, 2, 0).reshape(P, G * H)
    res[:, C_ROUTER:C_ROUTER + KH * E] = rows(a[_L0F + "W_router"].T, KH)
    res[:, C_ALOG:C_ALOG + NJ * NS] = rows(a[_L1A + "A_log"], NJ)
    res[:, C_LA1:C_LA1 + KH * RX] = rows(a[_L1F + "lora_a"], KH)
    v = res[:, C_VEC:]
    v[:, V_LP] = a[_L0A + "local_point"]
    v[:, V_B0:V_B0 + KH] = col(a[_L0F + "b_base"])
    v[:, V_CW:V_CW + NJ * KC] = rows(a[_L1A + "conv_w"], NJ)
    v[:, V_CB:V_CB + NJ] = col(a[_L1A + "conv_b"])
    v[:, V_BDT:V_BDT + NJ] = col(a[_L1A + "b_dt"])
    v[:, V_D:V_D + NJ] = col(a[_L1A + "D"])
    v[:, V_B1:V_B1 + KH] = col(a[_L1F + "b"])
    v[:, V_DISC:V_DISC + G] = a[_L0A + "discount_factor"]
    v[:, V_BR:V_BR + E] = a[_L0F + "b_router"]

    cst = np.zeros((P, NCONST), f32)
    cst[:, K_ID:K_ID + P] = np.eye(P)
    cst[:, K_MEAN:K_MEAN + P] = 1.0 / H
    for lo, n in ((0, RT), (RT, NS), (RT + NS, NS)):
        for twin in (0, P // 2):
            cst[lo:lo + n, K_RMS + twin + lo:K_RMS + twin + lo + n] = 1.0 / n
    for twin in (0, P // 2):
        cst[twin + RT:twin + P // 2, K_PICK:K_PICK + 2 * NS] = np.eye(2 * NS)
    cst[:, K_INV:K_INV + E] = 1.0 / np.arange(1, E + 1)
    cst[:, K_EPS], cst[:, K_EPS + 1] = 1e-5, 1e-6

    arrays = {
        "x_t": rows(a[_L0A + "hidden_states"][0].T, KH).reshape(P, KH, T), "chunks": chunks, "down_w": down_w,
        "gate_w": gate_w, "res": res, "lb1": a[_L1F + "lora_b"], "consts": cst,
    }
    arrays = {k: np.ascontiguousarray(w) for k, w in arrays.items()}
    nc = _bacc.Bacc("TRN2", target_bir_lowering=False, num_devices=1)
    args = [nc.dram_tensor(k, w.shape, F32, kind="ExternalInput").ap() for k, w in arrays.items()]
    out = nc.dram_tensor("out_t", (P, KH, T), F32, kind="ExternalOutput").ap()
    build(nc, *args, out)
    r = _run(nc, [arrays], core_ids=[0])
    got = r.results[0]["out_t"]
    return got.transpose(2, 1, 0).reshape(1, T, H)
```
